# Optimizing a Trainium2 kernel written in Bass

```python
import numpy as np
import jax
import jax.numpy as jnp

def _softmax(x, axis=-1):
    return jax.nn.softmax(x, axis=axis)

def _gelu(x):
    return jax.nn.gelu(x, approximate=True)

def _silu(x):
    return jax.nn.silu(x)

def _sigmoid(x):
    return jax.nn.sigmoid(x)

def _layernorm(x, axis=-1, eps=1e-05):
    m = jnp.mean(x, axis=axis, keepdims=True)
    v = jnp.var(x, axis=axis, keepdims=True)
    return (x - m) / jnp.sqrt(v + eps)

def _scatter_add(tgt, idx, src, axis=0):
    return tgt.at[idx].add(src)

def _segment_sum(src, seg, n):
    return jax.ops.segment_sum(src, seg, n)
kernel_name = 'mk_xattn_ffn_d1_seqx_r4_ae9dfa'

def setup_inputs(seed: int=0):
    np.random.seed(seed)
    _w = jnp.asarray

    def _rec_inputs():
        import jax
        import jax.numpy as jnp
        _rk = jax.random.key(seed)
        x = -0.0002928 + 1 * jax.random.normal(jax.random.fold_in(_rk, 1), (1, 2048, 256), jnp.float32)
        _lenS = 2048 - jax.random.randint(jax.random.fold_in(_rk, 7), (1,), 0, max(1, 2048 // 4) + 1, jnp.int32)
        _lenS2 = 1601 - jax.random.randint(jax.random.fold_in(_rk, 8), (1,), 0, max(1, 1601 // 4) + 1, jnp.int32)
        _ctx_768P = jax.random.normal(jax.random.fold_in(_rk, 11), (1, 16, 192), jnp.float32)
        _ctx_768c = jax.random.dirichlet(jax.random.fold_in(_rk, 511), 0.3 * jnp.ones((16,), jnp.float32), (1, 1601))
        _ctx_768t = jnp.einsum('bsk,bkd->bsd', _ctx_768c, _ctx_768P)
        _ctx_768t = _ctx_768t * jax.lax.rsqrt(jnp.mean(jnp.square(_ctx_768t)) + 1e-12) * 0.953939
        ctx_768 = 2.09791e-05 + 1.00001 * (_ctx_768t + 0.3 * jax.random.normal(jax.random.fold_in(_rk, 611), (1, 1601, 192), jnp.float32))
        _validS = jnp.arange(2048)[None, :] < _lenS[:, None]
        _validS2 = jnp.arange(1601)[None, :] < _lenS2[:, None]
        _causal = jnp.tril(jnp.ones((2048, 2048), dtype=bool))
        mask_BxS2_bf1 = jnp.ones((1, 1601), dtype=bool)
        return (x, ctx_768, mask_BxS2_bf1)
    x, ctx_768, mask_BxS2_bf1 = _rec_inputs()

    def _L0_xattn_setup():
        import jax, jax.numpy as jnp
        import numpy as np
        import math
        B, N, M = (4, 256, 256)
        DIM, CTX_DIM = (256, 192)
        HEADS, DIM_HEAD = (16, 64)
        INNER = HEADS * DIM_HEAD

        def layer_norm(t, g, eps=1e-05):
            mean = jnp.mean(t, axis=-1, keepdims=True)
            var = jnp.mean((t - mean) ** 2, axis=-1, keepdims=True)
            return (t - mean) * jax.lax.rsqrt(var + eps) * g
        key = jax.random.key(seed)
        ks = jax.random.split(key, 8)
        return {'x': jax.random.normal(ks[0], (B, N, DIM), jnp.float32), 'context': jax.random.normal(ks[1], (B, M, CTX_DIM), jnp.float32), 'mask': jnp.ones((B, M), dtype=bool), 'g_norm': jnp.ones((DIM,), jnp.float32), 'null_kv': jax.random.normal(ks[2], (2, DIM_HEAD), jnp.float32), 'Wq': jax.random.normal(ks[3], (DIM, INNER), jnp.float32) * DIM ** (-0.5), 'Wkv': jax.random.normal(ks[4], (CTX_DIM, 2 * INNER), jnp.float32) * CTX_DIM ** (-0.5), 'Wout': jax.random.normal(ks[5], (INNER, DIM), jnp.float32) * INNER ** (-0.5), 'g_out': jnp.ones((DIM,), jnp.float32)}
    _L0_xattn_all = _L0_xattn_setup()
    _L0_xattn_in = {k: v for k, v in _L0_xattn_all.items() if k in ('g_norm', 'null_kv', 'Wq', 'Wkv', 'Wout', 'g_out')}
    del _L0_xattn_all

    def _L0_ffn_setup():
        import jax, jax.numpy as jnp
        import numpy as np
        import math
        D_IN = 256
        FEATURES = (1024, 1024, 256)
        BATCH, SEQ = (8, 512)

        def _conn_dense(kernel_bool, x):
            w = jnp.where(kernel_bool, jnp.float32(1.0), jnp.float32(-1.0))
            return x @ w
        key = jax.random.key(seed)
        kx, kk0, kk1, kk2 = jax.random.split(key, 4)
        x = jax.random.normal(kx, (BATCH, SEQ, D_IN), dtype=jnp.float32)
        k0 = jax.random.randint(kk0, (2 * D_IN, FEATURES[0]), 0, 2).astype(jnp.bool_)
        k1 = jax.random.randint(kk1, (FEATURES[0], FEATURES[1]), 0, 2).astype(jnp.bool_)
        k2 = jax.random.randint(kk2, (FEATURES[1], FEATURES[2]), 0, 2).astype(jnp.bool_)
        s0 = jnp.asarray(1.0 / math.sqrt(2 * D_IN), dtype=jnp.float32)
        s1 = jnp.asarray(1.0 / math.sqrt(FEATURES[0]), dtype=jnp.float32)
        s2 = jnp.asarray(1.0 / math.sqrt(FEATURES[1]), dtype=jnp.float32)
        return {'x': x, 'k0': k0, 'k1': k1, 'k2': k2, 's0': s0, 's1': s1, 's2': s2}
    _L0_ffn_all = _L0_ffn_setup()
    _L0_ffn_in = {k: v for k, v in _L0_ffn_all.items() if k in ('k0', 'k1', 'k2', 's0', 's1', 's2')}
    del _L0_ffn_all
    return {'x': x, 'ctx_768': ctx_768, 'mask_BxS2_bf1': mask_BxS2_bf1, 'L0_xattn_g_norm': _L0_xattn_in['g_norm'], 'L0_xattn_null_kv': _L0_xattn_in['null_kv'], 'L0_xattn_Wq': _L0_xattn_in['Wq'], 'L0_xattn_Wkv': _L0_xattn_in['Wkv'], 'L0_xattn_Wout': _L0_xattn_in['Wout'], 'L0_xattn_g_out': _L0_xattn_in['g_out'], 'L0_ffn_k0': _L0_ffn_in['k0'], 'L0_ffn_k1': _L0_ffn_in['k1'], 'L0_ffn_k2': _L0_ffn_in['k2'], 'L0_ffn_s0': _L0_ffn_in['s0'], 'L0_ffn_s1': _L0_ffn_in['s1'], 'L0_ffn_s2': _L0_ffn_in['s2']}

def reference(x, ctx_768, mask_BxS2_bf1, L0_xattn_g_norm, L0_xattn_null_kv, L0_xattn_Wq, L0_xattn_Wkv, L0_xattn_Wout, L0_xattn_g_out, L0_ffn_k0, L0_ffn_k1, L0_ffn_k2, L0_ffn_s0, L0_ffn_s1, L0_ffn_s2):
    import jax
    import jax.numpy as jnp

    def _L0_xattn_ref(x, context, mask, g_norm, null_kv, Wq, Wkv, Wout, g_out):
        import jax, jax.numpy as jnp
        import numpy as np
        import math
        B, N, M = (4, 256, 256)
        DIM, CTX_DIM = (256, 192)
        HEADS, DIM_HEAD = (16, 64)
        INNER = HEADS * DIM_HEAD

        def layer_norm(t, g, eps=1e-05):
            mean = jnp.mean(t, axis=-1, keepdims=True)
            var = jnp.mean((t - mean) ** 2, axis=-1, keepdims=True)
            return (t - mean) * jax.lax.rsqrt(var + eps) * g
        b = x.shape[0]
        scale = DIM_HEAD ** (-0.5)
        sqrt_scale = math.sqrt(scale)
        x = layer_norm(x, g_norm)
        q = x @ Wq
        kv = context @ Wkv
        k, v = jnp.split(kv, 2, axis=-1)

        def to_heads(t):
            return t.reshape(b, t.shape[1], HEADS, DIM_HEAD).transpose(0, 2, 1, 3)
        q, k, v = (to_heads(q), to_heads(k), to_heads(v))
        nk = jnp.broadcast_to(null_kv[0], (b, HEADS, 1, DIM_HEAD))
        nv = jnp.broadcast_to(null_kv[1], (b, HEADS, 1, DIM_HEAD))
        k = jnp.concatenate([nk, k], axis=2)
        v = jnp.concatenate([nv, v], axis=2)
        q = q * sqrt_scale
        k = k * sqrt_scale
        sim = jnp.einsum('bhid,bhjd->bhij', q, k)
        max_neg = -jnp.finfo(sim.dtype).max
        full_mask = jnp.pad(mask, ((0, 0), (1, 0)), constant_values=True)
        sim = jnp.where(full_mask[:, None, None, :], sim, max_neg)
        attn = jax.nn.softmax(sim.astype(jnp.float32), axis=-1).astype(sim.dtype)
        out = jnp.einsum('bhij,bhjd->bhid', attn, v)
        out = out.transpose(0, 2, 1, 3).reshape(b, -1, INNER)
        out = out @ Wout
        return layer_norm(out, g_out)

    def _L0_ffn_ref(x, k0, k1, k2, s0, s1, s2):
        import jax, jax.numpy as jnp
        import numpy as np
        import math
        D_IN = 256
        FEATURES = (1024, 1024, 256)
        BATCH, SEQ = (8, 512)

        def _conn_dense(kernel_bool, x):
            w = jnp.where(kernel_bool, jnp.float32(1.0), jnp.float32(-1.0))
            return x @ w
        h = jnp.concatenate([x, -x], axis=-1)
        h = s0 * _conn_dense(k0, h)
        h = jax.nn.relu(h) * 2
        h = s1 * _conn_dense(k1, h)
        h = jax.nn.relu(h) * 2
        h = s2 * _conn_dense(k2, h)
        return h
    x = x + _L0_xattn_ref(_layernorm(x, axis=-1), ctx_768, mask_BxS2_bf1, L0_xattn_g_norm, L0_xattn_null_kv, L0_xattn_Wq, L0_xattn_Wkv, L0_xattn_Wout, L0_xattn_g_out)
    x = x + _L0_ffn_ref(_layernorm(x, axis=-1), L0_ffn_k0, L0_ffn_k1, L0_ffn_k2, L0_ffn_s0, L0_ffn_s1, L0_ffn_s2)
    return x

_drawn_inputs = setup_inputs


def setup_inputs(seed=0):
    import zlib

    import numpy as np

    out = dict(_drawn_inputs(seed))
    spreads = {'L0_xattn_g_norm': (1.0, 0.2), 'L0_xattn_g_out': (1.0, 0.2)}
    factors = {'L0_xattn_null_kv': 8.0}
    for name, (base, spread) in spreads.items():
        noise = np.random.default_rng([zlib.crc32(name.encode()), seed]).standard_normal(out[name].shape)
        drawn = base * np.exp(spread * noise) if base else spread * noise
        out[name] = jnp.asarray(drawn.astype(out[name].dtype))
    for name, factor in factors.items():
        out[name] = (out[name] * factor).astype(out[name].dtype)
    return out
```

```python
from contextlib import ExitStack

import concourse.bass as bass
from concourse import mybir

F32 = mybir.dt.float32
F32R = mybir.dt.float32r
U8 = mybir.dt.uint8
ALU = mybir.AluOpType
ACT = mybir.ActivationFunctionType
AX = mybir.AxisListType

P = 128
SEQ, DIM = 2048, 256
CTX, CDIM = 1601, 192
HEADS, HD = 16, 64
INNER = HEADS * HD
PAIRS = HEADS // 2
QT = SEQ // P
QB, QW = 4, 512
DC = DIM // P
KEYS = CTX + 1
KT = (KEYS + P - 1) // P
KPAD = KT * P
NULL_TILE, NULL_ROW = CTX // P, CTX % P
CAUG = CDIM + 2
C1 = CAUG - P
KCH = KPAD // 4
MXW = 402
MXH = 2 * MXW
FF = 1024
FK = FF // P
EPS = 1e-5
SCALE = float(HD) ** -0.5
MASKED = -30000.0
STEPS = QB * KT
RING = 4
CREDIT = 4

assert STEPS % RING == 0 and 4 * MXW >= KEYS and 4 * MXW <= KPAD and KPAD % 4 == 0


def plan_side(with_next):
    plan = {s: [] for s in range(STEPS + 1)}
    if with_next:
        for c in range(4):
            plan[c].append(("K", c))
            plan[4 + c].append(("Q", c))
        first, last, halves = 10, 46, 4 * QT
        done = 0
        for s in range(first, last + 1):
            upto = (s - first + 1) * halves // (last - first + 1)
            for j in range(done, upto):
                plan[s].append(("SA", j // (2 * QT), j % (2 * QT) // 2, j % 2))
            done = upto
        plan[30].append(("MX", 0))
        plan[49].append(("MX", 1))
    for qb in range(QB):
        plan[min(KT * (qb + 1) + 2, STEPS)].append(("L", qb))
    n = 0
    out = {}
    for s in range(STEPS + 1):
        out[s] = []
        for job in plan[s]:
            out[s].append((n, job))
            n += 1
    assert n % 2 == 0
    return out, n


def plan_first():
    jobs = [("K", c) for c in range(4)] + [("Q", c) for c in range(4)]
    jobs += [("SA", g, qt, half) for g in range(2) for qt in range(QT) for half in range(2)]
    jobs.insert(8 + 2 * QT + 6, ("MX", 0))
    jobs.append(("MX", 1))
    return list(enumerate(jobs))


SIDE, SIDE_N = plan_side(True)
LAST, LAST_N = plan_side(False)
FIRST = plan_first()


def plan_chain():
    roots, steps = [], []
    for k in range(8):
        if k < 4:
            roots.append(("A", k))
            steps.append(("A1", k))
        if 1 <= k < 5:
            roots.append(("B", k - 1))
            steps += [("B1", k - 1), ("B2", k - 1), ("B3", k - 1), ("B4", k - 1)]
        if 2 <= k < 6:
            steps.append(("C1", k - 2))
    return {r: n for n, r in enumerate(roots)}, {s: n + 1 for n, s in enumerate(steps)}


SQ, ORDER = plan_chain()
CHAIN_N = len(ORDER)
V_EARLY = 10


def hi_rows(g):
    return slice(HD * g, HD * g + HD)


def lo_rows(g):
    return slice(HD * (1 - g), HD * (1 - g) + HD)


def shift_row(g):
    return HD * (1 - g)


def consumed(s):
    return (KT - 1) * (s // KT) + max(s % KT, 1)


def xattn_ffn_kernel(nc, x, ctx_in, mask, g_norm, null_kv, wq, wkv, wout, g_out, k0, k1, k2, s0, s1, s2, out):
    v_dram = nc.dram_tensor("v_scratch", [PAIRS, P, KT, P], F32, kind="Internal").ap()
    o_dram = nc.dram_tensor("o_scratch", [PAIRS, P, SEQ], F32, kind="Internal").ap()

    with ExitStack() as es:
        def psum(name, shape):
            return es.enter_context(nc.psum_tensor(name, shape, F32))

        def sem(name):
            return es.enter_context(nc.semaphore(name))

        start = (nc.sbuf_base + 63) // 64 * 64
        at = {"": start}

        def sb(name, shape, dt=F32, region=""):
            size = 1
            for n in shape[1:]:
                size *= n
            size = (size * (1 if dt == U8 else 4) + 63) // 64 * 64
            t = nc.alloc_sbuf_tensor_at(name, shape, dt, offset=at[region])
            at[region] += size
            return t

        ident = sb("ident", [P, P])
        ones = sb("ones", [P, HD])
        epscol = sb("epscol", [P, 1])
        keybias = sb("keybias", [P, KT])
        gcol = sb("gcol", [P, DC])
        scol = sb("scol", [P, 3])
        s2x8 = sb("s2x8", [P, 1])
        mxh = sb("mxh", [P, 2, QT, 2])
        mx = sb("mx", [P, 2, QT])
        rowbuf = [sb(f"rowbuf{g}", [QT, P], F32R) for g in range(2)]
        wqp = [sb(f"wqp{u}", [P, DC, P]) for u in range(2)]
        wkp0 = [sb(f"wkp0_{u}", [P, P]) for u in range(2)]
        wkp1 = [sb(f"wkp1_{u}", [C1, P]) for u in range(2)]

        qdup, qrest, khl, krest = [[], []], [[], []], [[], []], [[], []]

        def operands(u):
            for g in range(2):
                qdup[u].append(sb(f"qdup{u}{g}", [P, SEQ], F32R))
                qrest[u].append(sb(f"qrest{u}{g}", [P, SEQ], F32R))
                khl[u].append(sb(f"khl{u}{g}", [P, KPAD], F32R))
                krest[u].append(sb(f"krest{u}{g}", [P, KPAD], F32R))

        at["tail0"] = at[""]
        operands(0)
        at["w02"] = at[""]
        xT = sb("xT", [P, DC, SEQ])
        at["head"] = at["tail1"] = at[""]
        operands(1)
        end_operands1 = at[""]
        cT0 = sb("cT0", [P, KPAD])
        cT1 = sb("cT1", [C1, KPAD])
        vp = [sb(f"vp{u}", [P, KT, P]) for u in range(2)]
        prob = [[sb(f"prob{g}{r}", [P, QW]) for r in range(RING)] for g in range(2)]
        acc = [[sb(f"acc{g}{r}", [P, QW]) for r in range(2)] for g in range(2)]
        oraw = [sb(f"oraw{r}", [P, QW]) for r in range(2)]
        rec = [sb(f"rec{r}", [P, QW]) for r in range(2)]
        onorm = [sb(f"onorm{r}", [P, QW]) for r in range(2)]
        end_all = at[""]
        assert end_all <= nc.sbuf_usable_end, end_all

        xs = sb("xs", [P, QT, DIM], region="head")
        ctxA = sb("ctxA", [P, KT, CAUG], region="head")
        wv0 = sb("wv0", [P, INNER], region="head")
        wv1 = sb("wv1", [C1, INNER], region="head")
        vsb = [sb(f"vsb{r}", [P, INNER], region="head") for r in range(2)]
        mask8 = sb("mask8", [KT, P], U8, region="head")
        maskf = sb("maskf", [KT, P], region="head")
        grow = sb("grow", [DC, P], region="head")
        m13 = sb("m13", [P, KT], region="head")
        st = sb("st", [P, 2, QT, 6], region="head")
        mv = sb("mv", [P, 2, QT, 2], region="head")
        sd = sb("sd", [P, 2, QT], region="head")
        rs = sb("rs", [P, 2, QT], region="head")
        assert at["head"] <= end_operands1

        wo_sb = sb("wo_sb", [P, PAIRS, DIM], region="tail0")
        k0raw = sb("k0raw", [P, 2 * DC, FF], U8, region="tail0")
        k1raw = sb("k1raw", [P, FK, FF], U8, region="tail0")
        k2raw = sb("k2raw", [P, FK, DIM], U8, region="tail0")
        otb = sb("otb", [P, PAIRS, QW], region="tail0")
        xres = sb("xres", [P, QT, DIM], region="tail0")
        gout = sb("gout", [P, DIM], region="tail0")
        assert at["tail0"] <= at["w02"]
        w0 = sb("w0", [P, DC, FF], F32R, region="w02")
        w2 = sb("w2", [P, FK, DIM], F32R, region="w02")
        assert at["w02"] <= at["tail1"]
        w1 = sb("w1", [P, FK, FF], F32R, region="tail1")
        yhi = sb("yhi", [P, DC, QW], F32R, region="tail1")
        ylo = sb("ylo", [P, DC, QW], F32R, region="tail1")
        h0hi = sb("h0hi", [P, FK, QW], F32R, region="tail1")
        h0lo = sb("h0lo", [P, FK, QW], F32R, region="tail1")
        h1hi = sb("h1hi", [P, FK, QW], F32R, region="tail1")
        h1lo = sb("h1lo", [P, FK, QW], F32R, region="tail1")
        hf = [sb(f"hf{r}", [P, QW], region="tail1") for r in range(2)]
        fT = [sb(f"fT{m}", [P, QW], region="tail1") for m in range(DC)]
        attn = [sb(f"attn{r}", [P, DIM], region="tail1") for r in range(2)]
        ysb = [sb(f"ysb{r}", [P, DIM], region="tail1") for r in range(2)]
        obuf = [sb(f"obuf{r}", [P, DIM], region="tail1") for r in range(2)]
        cst = [sb(f"cst{r}", [P, 2, 6], region="tail1") for r in range(2)]
        cmv = [sb(f"cmv{r}", [P, 2, 2], region="tail1") for r in range(2)]
        csd = [sb(f"csd{r}", [P, 2], region="tail1") for r in range(2)]
        crs = [sb(f"crs{r}", [P, 2], region="tail1") for r in range(2)]
        assert at["tail1"] <= end_all, (at["tail1"], end_all)

        ps_s = [psum(f"ps_s{g}", [P, 512]) for g in range(2)]
        ps_o = [psum(f"ps_o{r}", [P, 512]) for r in range(2)]
        ps_side = [psum(f"ps_side{r}", [P, 2, 512]) for r in range(2)]
        ps_c = ps_s
        ps_t = ps_o
        ps_f = [ps_side[0][:, 0, :], ps_side[0][:, 1, :], ps_side[1][:, 0, :]]

        ld_ctx, ld_mask, ld_x, ld_g = sem("ld_ctx"), sem("ld_mask"), sem("ld_x"), sem("ld_g")
        ld_wv, ld_null = sem("ld_wv"), sem("ld_null")
        init = sem("init")
        ld_gn, gT_made, gcol_made = sem("ld_gn"), sem("gT_made"), sem("gcol_made")
        ident_made = sem("ident_made")
        clear_ctx = sem("clear_ctx")
        null_set = sem("null_set")
        maskf_made, maskT_made, m13_made, keybias_made = sem("maskf_made"), sem("maskT_made"), sem("m13_made"), sem("keybias_made")
        ctx_masked = sem("ctx_masked")
        tr_made, tr_free = sem("tr_made"), sem("tr_free")
        vh_made, vh_free = sem("vh_made"), sem("vh_free")
        v_stored = [sem(f"v_stored{r}") for r in range(2)]
        ln_stats, ln_var, ln_sd, ln_rs, ln_out = sem("ln_stats"), sem("ln_var"), sem("ln_sd"), sem("ln_rs"), sem("ln_out")
        side_made = [sem(f"side_made{r}") for r in range(2)]
        side_free = [sem(f"side_free{r}") for r in range(2)]
        w_loaded = [sem(f"w_loaded{u}") for u in range(2)]
        v_loaded = sem("v_loaded")
        k_hi, k_lo, q_hi, q_lo = sem("k_hi"), sem("k_lo"), sem("q_hi"), sem("q_lo")
        k_copied, q_copied, shift_set = sem("k_copied"), sem("q_copied"), sem("shift_set")
        mx_made, row_made = sem("mx_made"), [sem("row_made0"), sem("row_made1")]
        s_made = [sem(f"s_made{g}") for g in range(2)]
        p_made = [sem(f"p_made{g}") for g in range(2)]
        pv_done = sem("pv_done")
        sum_done = [sem(f"sum_done{g}") for g in range(2)]
        o_copied = sem("o_copied")
        rec_made = sem("rec_made")
        norm_done = sem("norm_done")
        o_stored = [sem(f"o_stored{r}") for r in range(2)]
        ld_tail, ld_raw, ot_loaded = sem("ld_tail"), sem("ld_raw"), sem("ot_loaded")
        s2_made, w_small_made, w1_made = sem("s2_made"), sem("w_small_made"), [sem("w1_made_act"), sem("w1_made_dve")]
        c_made, c_free = sem("c_made"), sem("c_free")
        t_made, t_free = sem("t_made"), sem("t_free")
        f_made, f_free = sem("f_made"), sem("f_free")
        h_made, h_free = sem("h_made"), sem("h_free")
        split_step = sem("split_step")
        cv_made, csd_made = sem("cv_made"), sem("csd_made")
        cstep = sem("cstep")
        stood = sem("stood")
        y_made, yhi_made, y_split = sem("y_made"), sem("yhi_made"), sem("y_split")
        fT_made = sem("fT_made")
        res_made = sem("res_made")
        out_stored = [sem(f"out_stored{r}") for r in range(2)]

        block = es.enter_context(nc.Block())

        FIRST_SLOT = len(FIRST) // 2

        def slot_of(n, it, u, first):
            if first:
                return n % 2, n // 2
            return n % 2, FIRST_SLOT + (2 * it + u) * (SIDE_N // 2) + n // 2

        def pair_loop(eng, body):
            with eng.Fori(0, PAIRS // 2 - 1) as it:
                body(it, 0, True)
                body(it, 1, True)
            body(PAIRS // 2 - 1, 0, True)
            body(PAIRS // 2 - 1, 1, False)

        def turns_before(b):
            return 0 if isinstance(b, int) and b == 0 else 8 * b - 4

        def load_pair_weights(eng, it, u):
            c = (2 * it + u) * P
            eng.dma_start(wqp[u][:, :, :], wq[:, bass.ds(c, P)].rearrange("(c p) n -> p c n", p=P)).then_inc(w_loaded[u], 16)
            eng.dma_start(wkp0[u][:, :], wkv[0:P, bass.ds(c, P)]).then_inc(w_loaded[u], 16)
            eng.dma_start(wkp1[u][0:CDIM - P, :], wkv[P:CDIM, bass.ds(c, P)]).then_inc(w_loaded[u], 16)

        @block.sync
        def _(sp):
            sp.wait_ge(clear_ctx, 2)
            sp.dma_start(mask8[0:NULL_TILE, :], mask[0, 0:NULL_TILE * P].rearrange("(t p) -> t p", p=P)).then_inc(ld_mask, 16)
            sp.dma_start(mask8[NULL_TILE:KT, 0:NULL_ROW], mask[:, NULL_TILE * P:CTX]).then_inc(ld_mask, 16)
            sp.dma_start(ctxA[:, 0:NULL_TILE, 0:CDIM], ctx_in[0, 0:NULL_TILE * P, :].rearrange("(t p) c -> p t c", p=P)).then_inc(ld_ctx, 16)
            sp.dma_start(ctxA[0:NULL_ROW, NULL_TILE, 0:CDIM], ctx_in[0, NULL_TILE * P:CTX, :]).then_inc(ld_ctx, 16)
            sp.dma_start(xs[:, :, :], x[0].rearrange("(t p) d -> p t d", p=P)).then_inc(ld_x, 16)
            sp.dma_start(wv0[:, :], wkv[0:P, INNER:2 * INNER]).then_inc(ld_wv, 16)
            sp.dma_start(wv1[0:CDIM - P, :], wkv[P:CDIM, INNER:2 * INNER]).then_inc(ld_wv, 16)
            sp.dma_start(grow[:, :], g_norm.rearrange("(c p) -> c p", p=P)).then_inc(ld_gn, 16)
            sp.wait_ge(init, 4)
            row = CDIM - P
            sp.dma_start(wv1[row + 1:row + 2, :].rearrange("a (h d) -> a h d", h=HEADS),
                         null_kv[1:2, :].unsqueeze(1).broadcast_to([1, HEADS, HD])).then_inc(ld_null, 16)
            for u in range(2):
                sp.dma_start(wkp1[u][row:row + 1, :].rearrange("a (h d) -> a h d", h=2),
                             null_kv[0:1, :].unsqueeze(1).broadcast_to([1, 2, HD])).then_inc(ld_null, 16)
                load_pair_weights(sp, 0, u)
            for c, s in enumerate((s0, s1, s2)):
                sp.dma_start(scol[:, c:c + 1], s.unsqueeze(0).broadcast_to([P, 1])).then_inc(ld_g, 16)

            def store_v(kt):
                sp.wait_ge(vh_free, 2 * (kt + 1))
                sp.dma_start(v_dram[:, :, kt, :].rearrange("r p d -> p r d"),
                             vsb[kt % 2][:, :].rearrange("p (r d) -> p r d", d=P)).then_inc(v_stored[kt % 2], 16)

            def copies(it, u, kind):
                n = 2 * it + u
                if kind == "K":
                    sp.wait_ge(k_hi, 8 * n + 8)
                    for g in range(2):
                        sp.dma_start(krest[u][g][hi_rows(g), :].bitcast(F32), khl[u][g][hi_rows(g), :].bitcast(F32)).then_inc(k_copied, 16)
                else:
                    sp.wait_ge(q_hi, 8 * n + 8)
                    for g in range(2):
                        sp.dma_start(qdup[u][g][lo_rows(g), :].bitcast(F32), qdup[u][g][hi_rows(g), :].bitcast(F32)).then_inc(q_copied, 16)

            def set_shift(it, u, g):
                n = 2 * it + u
                sp.wait_ge(row_made[g], n + 1)
                r = shift_row(g)
                sp.dma_start(qrest[u][g][r:r + 1, :].bitcast(F32),
                             rowbuf[g][:, :].bitcast(F32)).then_inc(shift_set, 16)

            for kt in range(V_EARLY // 2):
                store_v(kt)
            copies(0, 0, "K")
            copies(0, 0, "Q")
            for kt in range(V_EARLY // 2, KT):
                store_v(kt)
            for r in range(2):
                sp.wait_ge(v_stored[r], 16 * ((KT + 1 - r) // 2))
            sp.dma_start(vp[0][:, :, :], v_dram[0]).then_inc(v_loaded, 16)
            set_shift(0, 0, 0)
            set_shift(0, 0, 1)

            def body(it, u, with_next):
                n = 2 * it + u
                nit, nu = (it, 1) if u == 0 else (it + 1, 0)

                def store_o(qb):
                    sp.wait_ge(norm_done, 2 + 4 * n + qb + 1)
                    sp.dma_start(o_dram[n, :, qb * QW:(qb + 1) * QW], onorm[qb % 2][:, :]).then_inc(o_stored[qb % 2], 16)

                if with_next:
                    sp.wait_ge(pv_done, CREDIT + STEPS * n)
                    sp.dma_start(vp[nu][:, :, :], v_dram[n + 1]).then_inc(v_loaded, 16)
                    if not (isinstance(it, int) and it == PAIRS // 2 - 1):
                        sp.wait_ge(q_lo, 8 * n + 8)
                        load_pair_weights(sp, it + 1, u)
                    copies(nit, nu, "K")
                    copies(nit, nu, "Q")
                else:
                    sp.wait_ge(pv_done, CREDIT + STEPS * n)
                    sp.dma_start(k0raw[:, :, :], k0.rearrange("(c p) n -> p c n", p=P)).then_inc(ld_raw, 16)
                    sp.dma_start(k2raw[:, :, :], k2.rearrange("(c p) n -> p c n", p=P)).then_inc(ld_raw, 16)
                    sp.dma_start(k1raw[:, :, :], k1.rearrange("(c p) n -> p c n", p=P)).then_inc(ld_raw, 16)
                    sp.dma_start(wo_sb[:, :, :], wout.rearrange("(c p) n -> p c n", p=P)).then_inc(ld_tail, 16)
                    sp.dma_start(xres[:, :, :], x[0].rearrange("(t p) d -> p t d", p=P)).then_inc(ld_tail, 16)
                    sp.dma_start(gout[:, :], g_out.unsqueeze(0).broadcast_to([P, DIM])).then_inc(ld_tail, 16)
                store_o(0)
                if with_next:
                    set_shift(nit, nu, 0)
                store_o(1)
                store_o(2)
                if with_next:
                    set_shift(nit, nu, 1)
                store_o(3)

            pair_loop(sp, body)

            for r in range(2):
                sp.wait_ge(o_stored[r], 16 * (1 + 2 * PAIRS))

            def load_ot(b):
                sp.dma_start(otb[:, :, :], o_dram[:, :, bass.ds(b * QW, QW)].rearrange("k p q -> p k q")).then_inc(ot_loaded, 16)

            def store_out(b):
                for t in range(4):
                    sp.wait_ge(res_made, 4 * b + t + 1)
                    sp.dma_start(out[0, bass.ds(b * QW + t * P, P), :], obuf[t % 2][:, :]).then_inc(out_stored[t % 2], 16)

            load_ot(0)
            sp.wait_ge(c_made, 4)
            load_ot(1)
            with sp.Fori(0, QB - 2) as b:
                sp.wait_ge(c_made, 4 * b + 8)
                load_ot(b + 2)
                store_out(b)
            store_out(QB - 2)
            store_out(QB - 1)
            for r in range(2):
                sp.wait_ge(out_stored[r], 16 * (1 + 2 * QB))

        @block.gpsimd
        def _(gp):
            gp.memset(ctxA[:, NULL_TILE, :], 0.0).then_inc(clear_ctx, 1)
            gp.memset(mask8[:, :], 0).then_inc(clear_ctx, 1)
            gp.memset(ident[:, :], 0.0).then_inc(ident_made, 1)
            gp.wait_ge(ident_made, 1)
            gp.affine_select(out=ident[:, :], in_=ident[:, :], compare_op=ALU.not_equal, fill=1.0, base=0,
                             pattern=[[-1, P]], channel_multiplier=1).then_inc(ident_made, 1)
            gp.memset(ones[:, :], 1.0).then_inc(init, 1)
            gp.wait_ge(init, 1)
            gp.wait_ge(ident_made, 2)
            gp.wait_ge(clear_ctx, 2)
            gp.memset(wv1[CDIM - P:C1, :], 0.0).then_inc(init, 1)
            for u in range(2):
                gp.memset(wkp1[u][CDIM - P:C1, :], 0.0).then_inc(init, 1)
            gp.wait_ge(init, 4)
            gp.memset(epscol[:, :], EPS).then_inc(init, 1)
            gp.memset(ctxA[:, 0:NULL_TILE, CDIM + 1:CAUG], 0.0).then_inc(null_set, 1)
            gp.wait_ge(clear_ctx, 1)
            gp.affine_select(out=ctxA[:, NULL_TILE, CDIM + 1:CAUG], in_=ctxA[:, NULL_TILE, CDIM + 1:CAUG],
                             compare_op=ALU.not_equal, fill=1.0, base=-NULL_ROW, pattern=[[0, 1]],
                             channel_multiplier=1).then_inc(null_set, 1)

            def clear_operands(u):
                gp.wait_ge(init, 5 + 6 * u)
                gp.wait_ge(null_set, 2)
                for g in range(2):
                    gp.wait_ge(init, 5 + 6 * u + 2 * g)
                    gp.memset(qrest[u][g][lo_rows(g), :].bitcast(F32), 0.0).then_inc(init, 1)
                    gp.memset(krest[u][g][lo_rows(g), :].bitcast(F32), 0.0).then_inc(init, 1)
                gp.wait_ge(init, 9 + 6 * u)
                for g in range(2):
                    gp.wait_ge(init, 9 + 6 * u + g)
                    r = shift_row(g)
                    gp.memset(krest[u][g][r:r + 1, :].bitcast(F32), 1.0).then_inc(init, 1)

            clear_operands(0)
            for r in range(2):
                gp.wait_ge(v_stored[r], 16 * ((KT + 1 - r) // 2))
            gp.wait_ge(tr_free, KT + QT)
            gp.wait_ge(vh_free, 2 * KT)
            gp.wait_ge(keybias_made, 2)
            clear_operands(1)

            gp.wait_ge(init, 17)

            def body(it, u, with_next):
                n = 2 * it + u
                for s in range(STEPS + 1):
                    if s < STEPS and s % KT:
                        qb, kt = s // KT, s % KT
                        a = acc[0][qb % 2]
                        done = CREDIT + (KT - 1) * (QB * n + qb) + kt - 1
                        gp.wait_ge(p_made[0], 1 + STEPS * n + s + 1)
                        gp.wait_ge(sum_done[0], done)
                        first = prob[0][(s - 1) % RING][:, :] if kt == 1 else a[:, :]
                        gp.tensor_tensor(a[:, :], first, prob[0][s % RING][:, :], ALU.add).then_inc(sum_done[0], 1)
                    for qb in range(QB):
                        if s == min(KT * (qb + 1) + 4, STEPS):
                            gp.wait_ge(rec_made, 4 * n + qb + 1)
                            gp.wait_ge(o_copied, 2 + 4 * n + qb + 1)
                            gp.wait_ge(o_stored[qb % 2], 16 * (1 + 2 * n + qb // 2))
                            gp.tensor_tensor(onorm[qb % 2][:, :], oraw[qb % 2][:, :], rec[qb % 2][:, :],
                                             ALU.mult).then_inc(norm_done, 1)

            gp.sem_inc(norm_done, 2)
            gp.sem_inc(o_stored[0], 16)
            gp.sem_inc(o_stored[1], 16)
            gp.sem_inc(sum_done[0], CREDIT)
            pair_loop(gp, body)

        @block.scalar
        def _(act):
            act.sem_inc(o_copied, 2)
            act.sem_inc(p_made[0], 1)
            act.sem_inc(p_made[1], 1)
            act.sem_inc(f_free, 3)

            def wait_side(n, it, u, first):
                slot, before = slot_of(n, it, u, first)
                act.wait_ge(side_made[slot], before + 1)
                return slot

            def side(n, job, it, u, first=False):
                if first:
                    nit, nu = 0, 0
                else:
                    nit, nu = (it, 1) if u == 0 else (it + 1, 0)
                nxt = 2 * nit + nu
                if job[0] == "K":
                    if job[1] == 0 and not first:
                        act.wait_ge(init, 17)
                    slot = wait_side(n, it, u, first)
                    cols = slice(job[1] * KCH, (job[1] + 1) * KCH)
                    for g in range(2):
                        act.activation(khl[nu][g][hi_rows(g), cols], ps_side[slot][hi_rows(g), 0, 0:KCH],
                                       ACT.Copy).then_inc(k_hi, 1)
                elif job[0] == "Q":
                    slot = wait_side(n, it, u, first)
                    cols = slice(job[1] * QW, (job[1] + 1) * QW)
                    for g in range(2):
                        act.activation(qdup[nu][g][hi_rows(g), cols], ps_side[slot][hi_rows(g), 0, :],
                                       ACT.Copy).then_inc(q_hi, 1)
                elif job[0] == "MX":
                    slot = wait_side(n, it, u, first)
                    g = job[1]
                    act.wait_ge(shift_set, 32 * nxt)
                    act.activation(rowbuf[g][:, :], ps_side[slot][0:QT, 0, 0:P], ACT.Copy,
                                   scale=-1.0).then_inc(row_made[g], 1)
                    act.wait_ge(row_made[g], nxt + 1)
                    act.sem_inc(side_free[slot], 1)

            for kt in range(KT):
                act.wait_ge(tr_made, kt + 1)
                act.activation(cT0[:, kt * P:(kt + 1) * P], ps_s[kt % 2][:, 0:P], ACT.Copy)
                act.activation(cT1[:, kt * P:(kt + 1) * P], ps_s[kt % 2][0:C1, P:2 * P], ACT.Copy).then_inc(tr_free, 1)

            def evac_v(h):
                kt, half = h // 2, h % 2
                act.wait_ge(vh_made, h + 1)
                if half == 0 and kt >= 2:
                    act.wait_ge(v_stored[kt % 2], 16 * (kt // 2))
                act.activation(vsb[kt % 2][:, half * 512:(half + 1) * 512], ps_o[h % 2][:, :],
                               ACT.Copy).then_inc(vh_free, 1)

            for h in range(V_EARLY // 2):
                evac_v(h)
            act.wait_ge(init, 5)
            for r in range(2):
                act.wait_ge(ln_var, r + 1)
                act.activation(sd[:, r, :], mv[:, r, :, 1], ACT.Sqrt, bias=epscol[:, :]).then_inc(ln_sd, 1)
            for h in range(V_EARLY // 2, V_EARLY):
                evac_v(h)
            for n, job in FIRST[0:4]:
                side(n, job, 0, 0, first=True)
            act.wait_ge(gcol_made, 1)
            for t in range(QT):
                i = KT + t
                act.wait_ge(tr_made, i + 1)
                for c in range(DC):
                    last = act.activation(xT[:, c, t * P:(t + 1) * P], ps_s[i % 2][:, c * P:(c + 1) * P],
                                          ACT.Copy, scale=gcol[:, c:c + 1])
                last.then_inc(tr_free, 1)
            h = V_EARLY
            for n, job in FIRST[4:]:
                side(n, job, 0, 0, first=True)
                if n >= 8 and n % 3 == 0 and h < 2 * KT:
                    evac_v(h)
                    h += 1
            assert h == 2 * KT

            def body(it, u, with_next):
                n = 2 * it + u
                plan = SIDE if with_next else LAST

                def copy_o(qb):
                    act.wait_ge(pv_done, CREDIT + STEPS * n + KT * (qb + 1))
                    act.wait_ge(norm_done, 4 * n + qb + 1)
                    act.activation(oraw[qb % 2][:, :], ps_o[qb % 2][:, :], ACT.Copy).then_inc(o_copied, 1)

                for s in range(STEPS):
                    kt = s % KT
                    freed = consumed(s - RING) + CREDIT if s >= RING else consumed(STEPS + s - RING) + CREDIT - (KT - 1) * QB
                    for g in range(2):
                        act.wait_ge(s_made[g], STEPS * n + s + 1)
                        act.wait_ge(pv_done, STEPS * n + s + 1)
                        act.wait_ge(sum_done[g], (KT - 1) * QB * n + freed)
                        act.activation(prob[g][s % RING][:, :], ps_s[g][:, :], ACT.Exp,
                                       bias=keybias[:, kt:kt + 1], scale=SCALE).then_inc(p_made[g], 1)
                    if s and kt == 0:
                        copy_o(s // KT - 1)
                    for j, job in plan[s]:
                        side(j, job, it, u)
                copy_o(QB - 1)

            act.wait_ge(keybias_made, 2)
            pair_loop(act, body)

            act.wait_ge(ld_raw, 48)
            act.wait_ge(pv_done, CREDIT + STEPS * PAIRS)
            for k in range(3):
                act.activation(w1[:, k, :], k1raw[:, k, :], ACT.Copy, scale=2.0, bias=-1.0).then_inc(w1_made[0], 1)

            def sqrt(i, r, n):
                act.wait_ge(cv_made, n + 1)
                act.activation(csd[i % 2][:, r:r + 1], cmv[i % 2][:, r, 1:2], ACT.Sqrt, bias=epscol[:, :]).then_inc(csd_made, 1)

            def chain(b, k):
                if k < 4:
                    sqrt(k, 0, 8 * b + SQ[("A", k)])
                if 1 <= k < 5:
                    sqrt(k - 1, 1, 8 * b + SQ[("B", k - 1)])
                if 4 <= k < 8:
                    t = k - 4
                    act.wait_ge(t_made, turns_before(b) + t + 1)
                    act.activation(yhi[:, :, t * P:(t + 1) * P], ps_t[t % 2][:, 0:DIM].rearrange("p (c q) -> p c q", c=DC),
                                   ACT.Copy).then_inc(yhi_made, 1)

            for k in range(8):
                chain(0, k)

            def relu(b, j, scale):
                act.wait_ge(f_made, 18 * b + j + 1)
                act.wait_ge(h_free, 16 * b + j + 1)
                act.activation(hf[j % 2][:, :], ps_f[j % 3], ACT.Relu, scale=scale).then_inc(h_made, 1)
                act.wait_ge(h_made, 16 * b + j + 1)
                act.sem_inc(f_free, 1)

            def tail(b, with_next):
                for m in range(8):
                    relu(b, m, scol[:, 0:1])
                for m in range(8):
                    relu(b, 8 + m, scol[:, 1:2])
                    if with_next:
                        chain(b + 1, m)
                for m in range(DC):
                    j = 16 + m
                    act.wait_ge(f_made, 18 * b + j + 1)
                    act.activation(fT[m][:, :], ps_f[j % 3], ACT.Copy, scale=s2x8[:, :]).then_inc(fT_made, 1)
                    act.wait_ge(fT_made, DC * b + m + 1)
                    act.sem_inc(f_free, 1)

            act.wait_ge(ld_g, 48)
            act.wait_ge(s2_made, 1)
            with act.Fori(0, QB - 1) as b:
                tail(b, True)
            tail(QB - 1, False)

        @block.vector
        def _(dve):
            dve.sem_inc(sum_done[1], CREDIT)
            dve.sem_inc(c_free, 2)
            dve.sem_inc(out_stored[0], 16)
            dve.sem_inc(out_stored[1], 16)
            dve.sem_inc(t_free, 2)
            dve.sem_inc(h_free, 2)
            dve.wait_ge(ld_mask, 32)
            dve.tensor_copy(maskf[:, :], mask8[:, :]).then_inc(maskf_made, 1)
            dve.wait_ge(maskT_made, 1)
            dve.tensor_copy(m13[:, :], ps_o[0][:, 0:KT]).then_inc(m13_made, 1)
            dve.wait_ge(m13_made, 1)
            dve.wait_ge(ld_ctx, 32)
            dve.wait_ge(null_set, 2)
            dve.tensor_scalar(ctxA[:, :, CDIM], m13[:, :], -1.0, 1.0, ALU.mult, ALU.add).then_inc(ctx_masked, 1)
            for kt in range(KT):
                dve.tensor_scalar(ctxA[:, kt, 0:CDIM], ctxA[:, kt, 0:CDIM], m13[:, kt:kt + 1], None,
                                  ALU.mult).then_inc(ctx_masked, 1)
            dve.tensor_tensor(keybias[:, :], m13[:, :], ctxA[:, :, CDIM + 1], ALU.add).then_inc(keybias_made, 1)
            dve.wait_ge(keybias_made, 1)
            dve.tensor_scalar(keybias[:, :], keybias[:, :], -1.0, -MASKED, ALU.add, ALU.mult).then_inc(keybias_made, 1)

            dve.wait_ge(gT_made, 1)
            dve.tensor_copy(gcol[:, :], ps_o[1][:, 0:DC]).then_inc(gcol_made, 1)

            dve.wait_ge(ld_x, 16)
            for r in range(2):
                for t in range(QT):
                    if r:
                        dve.wait_ge(ln_out, t + 1)
                    dve.bn_stats(st[:, r, t, :], xs[:, t, :]).then_inc(ln_stats, 1)
                dve.wait_ge(ln_stats, QT * (r + 1))
                for t in range(QT):
                    last = dve.bn_aggr(mv[:, r, t, :], st[:, r, t, :])
                last.then_inc(ln_var, 1)
                dve.wait_ge(ln_sd, r + 1)
                dve.reciprocal(rs[:, r, :], sd[:, r, :]).then_inc(ln_rs, 1)
                dve.wait_ge(ln_rs, r + 1)
                dve.wait_ge(ln_var, r + 1)
                for t in range(QT):
                    dve.tensor_scalar(xs[:, t, :], xs[:, t, :], mv[:, r, t, 0:1], rs[:, r, t:t + 1],
                                      ALU.subtract, ALU.mult).then_inc(ln_out, 1)

            def side(n, job, it, u, first=False):
                if first:
                    nit, nu = 0, 0
                else:
                    nit, nu = (it, 1) if u == 0 else (it + 1, 0)
                nxt = 2 * nit + nu
                slot, before = slot_of(n, it, u, first)
                if job[0] in "KQ":
                    c = job[1]
                    if job[0] == "K":
                        w, hi, whole, rest, lo_done = KCH, khl, k_hi, khl, k_lo
                    else:
                        w, hi, whole, rest, lo_done = QW, qdup, q_hi, qrest, q_lo
                    cols = slice(c * w, (c + 1) * w)
                    if job[0] == "Q" or c == 0:
                        dve.wait_ge(init, 11 if first else 17)
                    for g in range(2):
                        dve.wait_ge(whole, 8 * nxt + 2 * c + g + 1)
                        rows = lo_rows(g) if job[0] == "K" else hi_rows(g)
                        last = dve.tensor_tensor(rest[nu][g][rows, cols], ps_side[slot][hi_rows(g), 0, 0:w],
                                                 hi[nu][g][hi_rows(g), cols].bitcast(F32), ALU.subtract)
                        last.then_inc(lo_done, 1)
                    dve.wait_ge(lo_done, 8 * nxt + 2 * c + 2)
                    dve.sem_inc(side_free[slot], 1)
                elif job[0] == "SA":
                    _, g, qt, half = job
                    dve.wait_ge(side_made[slot], before + 1)
                    dve.reduce_max(mxh[:, g, qt, half:half + 1], ps_side[slot][:, :, 0:MXW], AX.XY).then_inc(side_free[slot], 1)
                    if (qt, half) == (QT - 1, 1):
                        dve.wait_ge(side_free[slot], before + 1)
                        dve.reduce_max(mx[:, g, :], mxh[:, g, :, :], AX.X).then_inc(mx_made, 1)
                elif job[0] == "L":
                    qb = job[1]
                    n_pair = 2 * it + u
                    dve.wait_ge(side_made[slot], before + 1)
                    dve.wait_ge(norm_done, 4 * n_pair + qb + 1)
                    dve.reciprocal(rec[qb % 2][:, :], ps_side[slot][:, 0, :]).then_inc(rec_made, 1)
                    dve.wait_ge(rec_made, 4 * n_pair + qb + 1)
                    dve.sem_inc(side_free[slot], 1)

            for n, job in FIRST:
                side(n, job, 0, 0, first=True)

            def body(it, u, with_next):
                n = 2 * it + u
                plan = SIDE if with_next else LAST
                for s in range(STEPS + 1):
                    for j, job in plan[s]:
                        side(j, job, it, u)
                    if s < STEPS and s % KT:
                        qb, kt = s // KT, s % KT
                        a = acc[1][qb % 2]
                        dve.wait_ge(p_made[1], 1 + STEPS * n + s + 1)
                        dve.wait_ge(sum_done[1], CREDIT + (KT - 1) * (QB * n + qb) + kt - 1)
                        first = prob[1][(s - 1) % RING][:, :] if kt == 1 else a[:, :]
                        dve.tensor_tensor(a[:, :], first, prob[1][s % RING][:, :], ALU.add).then_inc(sum_done[1], 1)
                    if not with_next and s == 20:
                        dve.wait_ge(ld_raw, 48)
                        dve.wait_ge(ld_g, 48)
                        dve.tensor_tensor(w0[:, :, :], k0raw[:, 0:DC, :], k0raw[:, DC:2 * DC, :], ALU.subtract).then_inc(w_small_made, 1)
                        dve.tensor_scalar(w2[:, :, :], k2raw[:, :, :], 2.0, -1.0, ALU.mult, ALU.add).then_inc(w_small_made, 1)
                        dve.tensor_scalar(s2x8[:, :], scol[:, 2:3], 8.0, None, ALU.mult).then_inc(s2_made, 1)

            pair_loop(dve, body)

            dve.wait_ge(pv_done, CREDIT + STEPS * PAIRS)
            dve.wait_ge(norm_done, 2 + 4 * PAIRS)
            for k in range(3, FK):
                dve.tensor_scalar(w1[:, k, :], k1raw[:, k, :], 2.0, -1.0, ALU.mult, ALU.add).then_inc(w1_made[1], 1)
            dve.wait_ge(ld_tail, 48)
    
            def chain(b, k):
                base = CHAIN_N * b

                def step(instruction, key):
                    instruction.then_inc(cstep, 1)
                    dve.wait_ge(cstep, base + ORDER[key])

                if k < 4:
                    i = k
                    dve.wait_ge(c_made, 4 * b + i + 1)
                    step(dve.bn_stats(cst[i % 2][:, 0, :], ps_c[i % 2][:, 0:DIM]), ("A1", i))
                    dve.sem_inc(stood, 1)
                    dve.bn_aggr(cmv[i % 2][:, 0, :], cst[i % 2][:, 0, :]).then_inc(cv_made, 1)
                if 1 <= k < 5:
                    i = k - 1
                    dve.wait_ge(csd_made, 8 * b + SQ[("A", i)] + 1)
                    step(dve.reciprocal(crs[i % 2][:, 0:1], csd[i % 2][:, 0:1]), ("B1", i))
                    dve.tensor_scalar(attn[i % 2][:, :], ps_c[i % 2][:, 0:DIM], cmv[i % 2][:, 0, 0:1], crs[i % 2][:, 0:1],
                                      ALU.subtract, ALU.mult).then_inc(c_free, 1)
                    dve.wait_ge(c_free, 2 + 4 * b + i + 1)
                    step(dve.tensor_tensor(attn[i % 2][:, :], attn[i % 2][:, :], gout[:, :], ALU.mult), ("B2", i))
                    xr = xres[:, bass.ds(4 * b + i, 1), :].rearrange("p a d -> p (a d)")
                    step(dve.tensor_tensor(xr, xr, attn[i % 2][:, :], ALU.add), ("B3", i))
                    dve.sem_inc(stood, 1)
                    step(dve.bn_stats(cst[i % 2][:, 1, :], xr), ("B4", i))
                    dve.sem_inc(stood, 1)
                    dve.bn_aggr(cmv[i % 2][:, 1, :], cst[i % 2][:, 1, :]).then_inc(cv_made, 1)
                if 2 <= k < 6:
                    i = k - 2
                    dve.wait_ge(csd_made, 8 * b + SQ[("B", i)] + 1)
                    step(dve.reciprocal(crs[i % 2][:, 1:2], csd[i % 2][:, 1:2]), ("C1", i))
                    xr = xres[:, bass.ds(4 * b + i, 1), :].rearrange("p a d -> p (a d)")
                    if i >= 2:
                        dve.wait_ge(t_made, turns_before(b) + i - 1)
                    dve.tensor_scalar(ysb[i % 2][:, :], xr, cmv[i % 2][:, 1, 0:1], crs[i % 2][:, 1:2],
                                      ALU.subtract, ALU.mult).then_inc(y_made, 1)
                if 4 <= k < 8:
                    t = k - 4
                    dve.wait_ge(yhi_made, 4 * b + t + 1)
                    dve.tensor_tensor(ylo[:, :, t * P:(t + 1) * P], ps_t[t % 2][:, 0:DIM].rearrange("p (c q) -> p c q", c=DC),
                                      yhi[:, :, t * P:(t + 1) * P].bitcast(F32), ALU.subtract).then_inc(y_split, 1)
                    dve.wait_ge(y_split, 4 * b + t + 1)
                    dve.sem_inc(t_free, 1)

            for k in range(8):
                chain(0, k)

            def split(b, j):
                hi, lo = (h0hi, h0lo) if j < 8 else (h1hi, h1lo)
                dve.wait_ge(h_made, 16 * b + j + 1)
                dve.tensor_copy(hi[:, j % 8, :], hf[j % 2][:, :]).then_inc(split_step, 1)
                dve.wait_ge(split_step, 16 * b + j + 1)
                dve.tensor_tensor(lo[:, j % 8, :], hf[j % 2][:, :], hi[:, j % 8, :].bitcast(F32),
                                  ALU.subtract).then_inc(h_free, 1)

            def tail(b, with_next):
                for j in range(8):
                    split(b, j)
                for j in range(8):
                    split(b, 8 + j)
                    if with_next:
                        chain(b + 1, j)
                for t in range(4):
                    dve.wait_ge(t_made, 8 * b + (8 if with_next else 4) + t + 1)
                    dve.wait_ge(out_stored[t % 2], 16 * (1 + 2 * b + t // 2))
                    xr = xres[:, bass.ds(4 * b + t, 1), :].rearrange("p a d -> p (a d)")
                    dve.tensor_tensor(obuf[t % 2][:, :], ps_t[t % 2][:, 0:DIM], xr, ALU.add).then_inc(res_made, 1)
                    dve.wait_ge(res_made, 4 * b + t + 1)
                    dve.sem_inc(t_free, 1)

            with dve.Fori(0, QB - 1) as b:
                tail(b, True)
            tail(QB - 1, False)

        @block.tensor
        def _(pe):
            pe.sem_inc(pv_done, CREDIT)

            pe.wait_ge(maskf_made, 1)
            pe.wait_ge(ident_made, 2)
            pe.transpose(ps_o[0][:, 0:KT], maskf[:, :], ident[0:KT, 0:KT]).then_inc(maskT_made, 1)
            pe.wait_ge(ld_gn, 16)
            pe.transpose(ps_o[1][:, 0:DC], grow[:, :], ident[0:DC, 0:DC]).then_inc(gT_made, 1)
            for kt in range(KT):
                pe.wait_ge(ctx_masked, kt + 2)
                if kt >= 2:
                    pe.wait_ge(tr_free, kt - 1)
                pe.transpose(ps_s[kt % 2][:, 0:P], ctxA[:, kt, 0:P], ident[:, :])
                pe.transpose(ps_s[kt % 2][0:C1, P:2 * P], ctxA[:, kt, P:CAUG], ident[:, :]).then_inc(tr_made, 1)

            def project_v(h):
                kt, half = h // 2, h % 2
                if h < 2:
                    pe.wait_ge(m13_made, 1)
                    pe.wait_ge(gcol_made, 1)
                else:
                    pe.wait_ge(vh_free, h - 1)
                keys, cols = slice(kt * P, (kt + 1) * P), slice(half * 512, (half + 1) * 512)
                pe.matmul(ps_o[h % 2][:, :], cT0[:, keys], wv0[:, cols], start=True, stop=False)
                pe.matmul(ps_o[h % 2][:, :], cT1[:, keys], wv1[:, cols], start=False, stop=True).then_inc(vh_made, 1)

            def side(n, job, it, u, first=False):
                if first:
                    nit, nu = 0, 0
                else:
                    nit, nu = (it, 1) if u == 0 else (it + 1, 0)
                nxt = 2 * nit + nu
                slot, before = slot_of(n, it, u, first)
                if not (first and before == 0):
                    pe.wait_ge(side_free[slot], before)
                ps = ps_side[slot]
                if job[0] == "K":
                    if job[1] == 0:
                        pe.wait_ge(w_loaded[nu], 48 * (nit + 1))
                    cols = slice(job[1] * KCH, (job[1] + 1) * KCH)
                    pe.matmul(ps[:, 0, 0:KCH], wkp0[nu][:, :], cT0[:, cols], start=True, stop=False)
                    pe.matmul(ps[:, 0, 0:KCH], wkp1[nu][:, :], cT1[:, cols], start=False, stop=True).then_inc(side_made[slot], 1)
                elif job[0] == "Q":
                    cols = slice(job[1] * QW, (job[1] + 1) * QW)
                    for c in range(DC):
                        last = pe.matmul(ps[:, 0, :], wqp[nu][:, c, :], xT[:, c, cols], start=(c == 0), stop=(c == DC - 1))
                    last.then_inc(side_made[slot], 1)
                elif job[0] == "SA":
                    _, g, qt, half = job
                    if (g, qt, half) == (0, 0, 0):
                        pe.wait_ge(q_copied, 32 * (nxt + 1))
                        pe.wait_ge(k_lo, 8 * (nxt + 1))
                    for j in range(2):
                        cols = slice(half * MXH + j * MXW, half * MXH + (j + 1) * MXW)
                        last = pe.matmul(ps[:, j, 0:MXW], qdup[nu][g][:, qt * P:(qt + 1) * P], khl[nu][g][:, cols],
                                         start=True, stop=True)
                    last.then_inc(side_made[slot], 1)
                elif job[0] == "MX":
                    g = job[1]
                    pe.wait_ge(mx_made, 2 * nxt + g + 1)
                    pe.transpose(ps[0:QT, 0, 0:P], mx[:, g, :], ident[:, :]).then_inc(side_made[slot], 1)
                else:
                    qb = job[1]
                    for g in range(2):
                        pe.wait_ge(sum_done[g], CREDIT + (KT - 1) * (QB * (2 * it + u) + qb + 1))
                        last = pe.matmul(ps[g * HD:(g + 1) * HD, 0, :], ones[:, :], acc[g][qb % 2][:, :], start=True, stop=True)
                    last.then_inc(side_made[slot], 1)

            pe.wait_ge(tr_free, KT)
            pe.wait_ge(ld_wv, 32)
            pe.wait_ge(ld_null, 48)
            for h in range(V_EARLY):
                project_v(h)
            for n, job in FIRST[0:4]:
                side(n, job, 0, 0, first=True)
            for t in range(QT):
                i = KT + t
                pe.wait_ge(ln_out, QT + t + 1)
                pe.wait_ge(tr_free, i - 1)
                for c in range(DC):
                    last = pe.transpose(ps_s[i % 2][:, c * P:(c + 1) * P], xs[:, t, c * P:(c + 1) * P], ident[:, :])
                last.then_inc(tr_made, 1)
            pe.wait_ge(tr_free, KT + QT)
            h = V_EARLY
            for n, job in FIRST[4:]:
                side(n, job, 0, 0, first=True)
                if n >= 8 and n % 3 == 0 and h < 2 * KT:
                    project_v(h)
                    h += 1
            pe.wait_ge(vh_free, 2 * KT)

            def body(it, u, with_next):
                n = 2 * it + u
                plan = SIDE if with_next else LAST
                pe.wait_ge(k_copied, 32 * (n + 1))
                pe.wait_ge(q_lo, 8 * (n + 1))
                pe.wait_ge(shift_set, 32 * (n + 1))
                pe.wait_ge(v_loaded, 16 * (n + 1))
                if u == 0:
                    pe.wait_ge(init, 11)
                else:
                    pe.wait_ge(init, 17)

                def values(s):
                    qb, kt = s // KT, s % KT
                    if kt == 0:
                        pe.wait_ge(o_copied, 4 * n + qb + 1)
                    for g in range(2):
                        pe.wait_ge(p_made[g], 1 + STEPS * n + s + 1)
                        last = pe.matmul(ps_o[qb % 2][hi_rows(g), :], vp[u][:, kt, hi_rows(g)], prob[g][s % RING][:, :],
                                         start=(kt == 0), stop=(kt == KT - 1))
                    last.then_inc(pv_done, 1)

                for s in range(STEPS):
                    qb, kt = s // KT, s % KT
                    qs, ks = slice(qb * QW, (qb + 1) * QW), slice(kt * P, (kt + 1) * P)
                    for g in range(2):
                        pe.wait_ge(p_made[g], 1 + STEPS * n + s)
                        pe.matmul(ps_s[g][:, :], khl[u][g][:, ks], qdup[u][g][:, qs], start=True, stop=False)
                        pe.matmul(ps_s[g][:, :], krest[u][g][:, ks], qrest[u][g][:, qs], start=False,
                                  stop=True).then_inc(s_made[g], 1)
                    for j, job in plan[s]:
                        side(j, job, it, u)
                    if s:
                        values(s - 1)
                values(STEPS - 1)
                for j, job in plan[STEPS]:
                    side(j, job, it, u)

            pair_loop(pe, body)

            pe.wait_ge(ld_tail, 48)
            pe.wait_ge(o_copied, 2 + 4 * PAIRS)
            pe.wait_ge(side_free[0], FIRST_SLOT + (PAIRS - 1) * (SIDE_N // 2) + LAST_N // 2)
            pe.wait_ge(side_free[1], FIRST_SLOT + (PAIRS - 1) * (SIDE_N // 2) + LAST_N // 2)

            def project_out(b, t):
                if t == 0:
                    pe.wait_ge(ot_loaded, 16 * (b + 1))
                pe.wait_ge(c_free, 4 * b + t + 1)
                for k in range(PAIRS):
                    last = pe.matmul(ps_c[t % 2][:, 0:DIM], otb[:, k, t * P:(t + 1) * P], wo_sb[:, k, :],
                                     start=(k == 0), stop=(k == PAIRS - 1))
                last.then_inc(c_made, 1)

            def turn_y(b, t):
                pe.wait_ge(y_made, 4 * b + t + 1)
                pe.wait_ge(t_free, turns_before(b) + t + 1)
                for c in range(DC):
                    last = pe.transpose(ps_t[t % 2][:, c * P:(c + 1) * P], ysb[t % 2][:, c * P:(c + 1) * P], ident[:, :])
                last.then_inc(t_made, 1)

            def chain(b, k):
                if k < 4:
                    project_out(b, k)
                else:
                    turn_y(b, k - 4)

            for k in range(8):
                chain(0, k)
            pe.wait_ge(w_small_made, 2)

            def layer(b, j, weights, m, hi, lo, depth):
                pe.wait_ge(f_free, 18 * b + j + 1)
                for k in range(depth):
                    for part in (hi, lo):
                        last = pe.matmul(ps_f[j % 3], weights[:, k, m * P:(m + 1) * P], part[:, k, :],
                                         start=(k == 0 and part is hi), stop=(k == depth - 1 and part is lo))
                last.then_inc(f_made, 1)

            def tail(b, with_next):
                pe.wait_ge(y_split, 4 * b + 4)
                for m in range(8):
                    layer(b, m, w0, m, yhi, ylo, DC)
                pe.wait_ge(w1_made[0], 3)
                pe.wait_ge(w1_made[1], FK - 3)
                pe.wait_ge(h_free, 2 + 16 * b + 8)
                for m in range(8):
                    layer(b, 8 + m, w1, m, h0hi, h0lo, FK)
                    if with_next:
                        chain(b + 1, m)
                pe.wait_ge(h_free, 2 + 16 * b + 16)
                for m in range(DC):
                    layer(b, 16 + m, w2, m, h1hi, h1lo, FK)
                pe.wait_ge(fT_made, DC * (b + 1))
                for t in range(4):
                    pe.wait_ge(t_free, 8 * b + (8 if with_next else 4) + t + 1)
                    for c in range(DC):
                        last = pe.transpose(ps_t[t % 2][:, c * P:(c + 1) * P], fT[c][:, t * P:(t + 1) * P], ident[:, :])
                    last.then_inc(t_made, 1)

            with pe.Fori(0, QB - 1) as b:
                tail(b, True)
            tail(QB - 1, False)


_INS = ["x", "ctx_768", "mask_BxS2_bf1", "L0_xattn_g_norm", "L0_xattn_null_kv", "L0_xattn_Wq", "L0_xattn_Wkv",
        "L0_xattn_Wout", "L0_xattn_g_out", "L0_ffn_k0", "L0_ffn_k1", "L0_ffn_k2", "L0_ffn_s0", "L0_ffn_s1", "L0_ffn_s2"]


def kernel(**inputs):
    import numpy as np
    import concourse.bacc as bacc
    from concourse.bass_utils import run_bass_kernel_spmd

    nc = bacc.Bacc("TRN2", target_bir_lowering=False, num_devices=1)
    arrays, args = {}, []
    for name in _INS:
        a = np.ascontiguousarray(inputs[name])
        if a.ndim == 0:
            a = a.reshape(1)
        arrays[f"in_{name}"] = a
        args.append(nc.dram_tensor(f"in_{name}", a.shape, mybir.dt.from_np(a.dtype), kind="ExternalInput").ap())
    out = nc.dram_tensor("out", (1, SEQ, DIM), F32, kind="ExternalOutput").ap()
    xattn_ffn_kernel(nc, *args, out)
    r = run_bass_kernel_spmd(nc, [arrays], core_ids=[0])
    return r.results[0]["out"]
```

```python
from contextlib import ExitStack

import concourse.bass as bass
from concourse import mybir

F32 = mybir.dt.float32
F32R = mybir.dt.float32r
U8 = mybir.dt.uint8
ALU = mybir.AluOpType
ACT = mybir.ActivationFunctionType
AX = mybir.AxisListType

P = 128
SEQ, DIM = 2048, 256
CTX, CDIM = 1601, 192
HEADS, HD = 16, 64
INNER = HEADS * HD
PAIRS = HEADS // 2
QT = SEQ // P
QB, QW = 4, 512
DC = DIM // P
KEYS = CTX + 1
KT = (KEYS + P - 1) // P
KPAD = KT * P
NULL_TILE, NULL_ROW = CTX // P, CTX % P
CAUG = CDIM + 2
C1 = CAUG - P
KCH = KPAD // 4
MXW = 402
MXH = 2 * MXW
FF = 1024
FK = FF // P
EPS = 1e-5
SCALE = float(HD) ** -0.5
MASKED = -30000.0
STEPS = QB * KT
RING = 4
CREDIT = 4

assert STEPS % RING == 0 and 4 * MXW >= KEYS and 4 * MXW <= KPAD and KPAD % 4 == 0


L_STEPS = {qb: KT * (qb + 1) + 2 for qb in range(QB - 1)}


def plan_side(first, last):
    plan = {s: [] for s in range(STEPS + 1)}
    if not first:
        plan[2].append(("LP", QB - 1))
    for qb, s in L_STEPS.items():
        plan[s].append(("L", qb))
    if last:
        plan[STEPS].append(("L", QB - 1))
    else:
        for c in range(4):
            plan[c].append(("K", c))
            plan[4 + c].append(("Q", c))
        busy = [x for s in L_STEPS.values() for x in (s, s + 1)]
        steps = [s for s in range(SA_FIRST, SA_LAST + 1) if s not in busy]
        halves = 4 * QT
        for i, s in enumerate(steps):
            for j in range(i * halves // len(steps), (i + 1) * halves // len(steps)):
                plan[s].append(("SA", j // (2 * QT), j % (2 * QT) // 2, j % 2))
        plan[31].append(("MX", 0))
        plan[50].append(("MX", 1))
    n = 0
    out = {}
    for s in range(STEPS + 1):
        out[s] = []
        for job in plan[s]:
            out[s].append((n, job))
            n += 1
    return out, n


def plan_head():
    values = iter([("V", h, part) for h in range(2 * KT) for part in range(2)])
    order = [("CT", i) for i in range(CT_N)] + [("K", c) for c in range(4)]
    order += [next(values) for _ in range(V_FIRST)]

    def queries(c):
        return [("XT", 2 * c), next(values), ("XT", 2 * c + 1), next(values), ("Q", c), next(values)]

    order += queries(0) + queries(1)
    n = 0
    for c in range(4):
        for g in range(2):
            for qt in range(4 * c, 4 * c + 4):
                for half in range(2):
                    if (c, g, qt, half) == (3, 1, 13, 1):
                        order.append(("MX", 0))
                    order.append(("SA", g, qt, half))
                    n += 1
                    if n % 7 in (0, 2, 4, 6):
                        order += [job for job in (next(values, None),) if job]
        if c + 2 < 4:
            order += queries(c + 2)
    order.append(("MX", 1))
    assert not list(values)
    out, n = [], 0
    for job in order:
        if job[0] in ("CT", "XT", "V"):
            out.append((None, job))
        else:
            out.append((n, job))
            n += 1
    return out, n


CT_N = (KT + 1) // 2
XT_N = QT // 2
V_FIRST = 7
SA_FIRST, SA_LAST = 10, 47
PLAN_FIRST, FIRST_N = plan_side(True, False)
PLAN, SIDE_N = plan_side(False, False)
PLAN_LAST, LAST_N = plan_side(False, True)
HEAD, HEAD_N = plan_head()
BEFORE_1 = HEAD_N + FIRST_N
TOTAL_N = BEFORE_1 + (PAIRS - 2) * SIDE_N + LAST_N
assert SIDE_N % 2 == 0 and TOTAL_N % 2 == 0

def gpsimd_sums(g, s, last):
    if g == 0:
        return True
    return s % 3 == 0 if last else SA_FIRST <= s <= SA_LAST + 2 and s % 2 == 0


def plan_chain():
    roots, steps = [], []
    for k in range(8):
        if k < 4:
            roots.append(("A", k))
            steps.append(("A1", k))
        if 1 <= k < 5:
            roots.append(("B", k - 1))
            steps += [("B1", k - 1), ("B2", k - 1), ("B3", k - 1), ("B4", k - 1)]
        if 2 <= k < 6:
            steps.append(("C1", k - 2))
    return {r: n for n, r in enumerate(roots)}, {s: n + 1 for n, s in enumerate(steps)}


SQ, ORDER = plan_chain()
CHAIN_N = len(ORDER)
def hi_rows(g):
    return slice(HD * g, HD * g + HD)


def lo_rows(g):
    return slice(HD * (1 - g), HD * (1 - g) + HD)


def shift_row(g):
    return HD * (1 - g)


def consumed(s):
    return (KT - 1) * (s // KT) + max(s % KT, 1)


def xattn_ffn_kernel(nc, x, ctx_in, mask, g_norm, null_kv, wq, wkv, wout, g_out, k0, k1, k2, s0, s1, s2, out):
    v_dram = nc.dram_tensor("v_scratch", [PAIRS, P, KT, P], F32, kind="Internal").ap()
    o_dram = nc.dram_tensor("o_scratch", [PAIRS, P, SEQ], F32, kind="Internal").ap()

    with ExitStack() as es:
        def psum(name, shape):
            return es.enter_context(nc.psum_tensor(name, shape, F32))

        def sem(name):
            return es.enter_context(nc.semaphore(name))

        start = (nc.sbuf_base + 63) // 64 * 64
        at = {"": start}

        def sb(name, shape, dt=F32, region=""):
            size = 1
            for n in shape[1:]:
                size *= n
            size = (size * (1 if dt == U8 else 4) + 63) // 64 * 64
            t = nc.alloc_sbuf_tensor_at(name, shape, dt, offset=at[region])
            at[region] += size
            return t

        ident = sb("ident", [P, P])
        ones = sb("ones", [P, HD])
        epscol = sb("epscol", [P, 1])
        eps2col = sb("eps2col", [P, 1])
        keybias = sb("keybias", [P, KT])
        gcol = sb("gcol", [P, DC])
        scol = sb("scol", [P, 3])
        s2x8 = sb("s2x8", [P, 1])
        mxh = sb("mxh", [P, 2, QT, 2])
        mx = sb("mx", [P, 2, QT])
        rowbuf = [sb(f"rowbuf{g}", [QT, P], F32R) for g in range(2)]
        wqp = [sb(f"wqp{u}", [P, DC, P]) for u in range(2)]
        wkp0 = [sb(f"wkp0_{u}", [P, P]) for u in range(2)]
        wkp1 = [sb(f"wkp1_{u}", [C1, P]) for u in range(2)]

        qdup, qrest, khl, krest = [[], []], [[], []], [[], []], [[], []]

        def operands(u):
            for g in range(2):
                qdup[u].append(sb(f"qdup{u}{g}", [P, SEQ], F32R))
                qrest[u].append(sb(f"qrest{u}{g}", [P, SEQ], F32R))
                khl[u].append(sb(f"khl{u}{g}", [P, KPAD], F32R))
                krest[u].append(sb(f"krest{u}{g}", [P, KPAD], F32R))

        at["tail0"] = at[""]
        operands(0)
        at["w02"] = at[""]
        xT = sb("xT", [P, DC, SEQ])
        at["head"] = at["tail1"] = at[""]
        operands(1)
        end_operands1 = at[""]
        cT0 = sb("cT0", [P, KPAD])
        cT1 = sb("cT1", [C1, KPAD])
        vp = [sb(f"vp{u}", [P, KT, P]) for u in range(2)]
        prob = [[sb(f"prob{g}{r}", [P, QW]) for r in range(RING)] for g in range(2)]
        acc = [[sb(f"acc{g}{r}", [P, QW]) for r in range(2)] for g in range(2)]
        oraw = [sb(f"oraw{r}", [P, QW]) for r in range(2)]
        rec = [sb(f"rec{r}", [P, QW]) for r in range(2)]
        onorm = [sb(f"onorm{r}", [P, QW]) for r in range(2)]
        end_all = at[""]
        assert end_all <= nc.sbuf_usable_end, end_all

        xs = sb("xs", [P, QT, DIM], region="head")
        ctxA = sb("ctxA", [P, KT, CAUG], region="head")
        wv0 = sb("wv0", [P, INNER], region="head")
        wv1 = sb("wv1", [C1, INNER], region="head")
        vsb = [sb(f"vsb{r}", [P, INNER], region="head") for r in range(2)]
        mask8 = sb("mask8", [KT, P], U8, region="head")
        maskf = sb("maskf", [KT, P], region="head")
        grow = sb("grow", [DC, P], region="head")
        m13 = sb("m13", [P, KT], region="head")
        st = sb("st", [P, QT, 6], region="head")
        mv = sb("mv", [P, QT, 2], region="head")
        sd = sb("sd", [P, QT], region="head")
        rs = sb("rs", [P, QT], region="head")
        assert at["head"] <= end_operands1

        wo_sb = sb("wo_sb", [P, PAIRS, DIM], region="tail0")
        k0raw = sb("k0raw", [P, 2 * DC, FF], U8, region="tail0")
        k1raw = sb("k1raw", [P, FK, FF], U8, region="tail0")
        k2raw = sb("k2raw", [P, FK, DIM], U8, region="tail0")
        otb = sb("otb", [P, PAIRS, QW], region="tail0")
        xres = sb("xres", [P, QT, DIM], region="tail0")
        gout = sb("gout", [P, DIM], region="tail0")
        at["small"] = at["tail0"]
        end_operands0 = at["w02"]
        w0 = sb("w0", [P, DC, FF], F32R, region="w02")
        w2 = sb("w2", [P, FK, DIM], F32R, region="w02")
        assert at["w02"] <= at["tail1"]
        ysb = [sb(f"ysb{r}", [P, DIM], region="tail1") for r in range(2)]
        w1 = sb("w1", [P, FK, FF], F32R, region="tail1")
        yhi = sb("yhi", [P, DC, QW], F32R, region="tail1")
        ylo = sb("ylo", [P, DC, QW], F32R, region="tail1")
        h0hi = sb("h0hi", [P, FK, QW], F32R, region="tail1")
        h0lo = sb("h0lo", [P, FK, QW], F32R, region="tail1")
        h1hi = sb("h1hi", [P, FK, QW], F32R, region="tail1")
        h1lo = sb("h1lo", [P, FK, QW], F32R, region="tail1")
        hf = [sb(f"hf{r}", [P, QW], region="tail1") for r in range(2)]
        fT = [sb(f"fT{m}", [P, QW], region="tail1") for m in range(DC)]
        attn = [sb(f"attn{r}", [P, DIM], region="small") for r in range(2)]
        obuf = [sb(f"obuf{r}", [P, DIM], region="tail1") for r in range(2)]
        cst = [sb(f"cst{r}", [P, 2, 6], region="small") for r in range(2)]
        cmv = [sb(f"cmv{r}", [P, 2, 2], region="small") for r in range(2)]
        csd = [sb(f"csd{r}", [P, 2], region="small") for r in range(2)]
        crs = [sb(f"crs{r}", [P, 2], region="small") for r in range(2)]
        assert at["tail1"] <= end_all, (at["tail1"], end_all)
        assert at["small"] <= end_operands0, (at["small"], end_operands0)

        ps_s = [psum(f"ps_s{g}", [P, 512]) for g in range(2)]
        ps_o = [psum(f"ps_o{r}", [P, 512]) for r in range(2)]
        ps_side = [psum(f"ps_side{r}", [P, 2, 512]) for r in range(2)]
        ps_c = ps_s
        ps_t = ps_o
        ps_f = [ps_side[0][:, 0, :], ps_side[0][:, 1, :], ps_side[1][:, 0, :]]

        ld_ctx, ld_mask, ld_x, ld_g = sem("ld_ctx"), sem("ld_mask"), [sem(f"ld_x{c}") for c in range(4)], sem("ld_g")
        ld_wv, ld_null = sem("ld_wv"), sem("ld_null")
        init = sem("init")
        ld_gn, gT_made, gcol_made = sem("ld_gn"), sem("gT_made"), sem("gcol_made")
        ident_made = sem("ident_made")
        clear_ctx = sem("clear_ctx")
        null_set = sem("null_set")
        maskf_made, maskT_made, m13_made, keybias_made = sem("maskf_made"), sem("maskT_made"), sem("m13_made"), sem("keybias_made")
        flag_made = sem("flag_made")
        ctx_masked = sem("ctx_masked")
        tr_made, tr_free = sem("tr_made"), sem("tr_free")
        vh_made, vh_free = sem("vh_made"), sem("vh_free")
        v_stored = [sem(f"v_stored{r}") for r in range(2)]
        ln_stats, ln_var, ln_sd, ln_rs, ln_out = sem("ln_stats"), sem("ln_var"), sem("ln_sd"), sem("ln_rs"), sem("ln_out")
        side_made = [sem(f"side_made{r}") for r in range(2)]
        side_free = [sem(f"side_free{r}") for r in range(2)]
        w_loaded = [sem(f"w_loaded{u}") for u in range(2)]
        v_loaded = sem("v_loaded")
        k_hi, k_lo, q_hi, q_lo = sem("k_hi"), sem("k_lo"), sem("q_hi"), sem("q_lo")
        k_copied, q_copied, shift_set = sem("k_copied"), sem("q_copied"), sem("shift_set")
        q0_copied = [sem(f"q0_copied{c}") for c in range(4)]
        mx_made, row_made = sem("mx_made"), [sem("row_made0"), sem("row_made1")]
        s_made = [sem(f"s_made{g}") for g in range(2)]
        p_made = [sem(f"p_made{g}") for g in range(2)]
        pv_done = sem("pv_done")
        sum_done = [sem(f"sum_done{g}") for g in range(2)]
        o_copied = sem("o_copied")
        rec_made = sem("rec_made")
        norm_done = sem("norm_done")
        o_stored = [sem(f"o_stored{r}") for r in range(2)]
        ld_tail, ld_raw, ot_loaded = sem("ld_tail"), sem("ld_raw"), sem("ot_loaded")
        s2_made, w_small_made, w1_made = sem("s2_made"), sem("w_small_made"), [sem("w1_made_act"), sem("w1_made_gpsimd")]
        c_made, c_free = sem("c_made"), sem("c_free")
        t_made, t_free = sem("t_made"), sem("t_free")
        f_made, f_free = sem("f_made"), sem("f_free")
        h_made, h_free = sem("h_made"), sem("h_free")
        split_step = sem("split_step")
        cv_made, csd_made = sem("cv_made"), sem("csd_made")
        cstep = sem("cstep")
        stood = sem("stood")
        y_made, yhi_made, y_split = sem("y_made"), sem("yhi_made"), sem("y_split")
        fT_made = sem("fT_made")
        res_made = sem("res_made")
        out_stored = [sem(f"out_stored{r}") for r in range(2)]

        block = es.enter_context(nc.Block())

        def slot_of(j, pair):
            if pair is None:
                return j % 2, j // 2
            if isinstance(pair[0], int) and pair[0] == 0:
                j += HEAD_N
                return j % 2, j // 2
            j += BEFORE_1
            return j % 2, j // 2 + (pair[0] - 1) * (SIDE_N // 2)

        FIRST_PAIR, LAST_PAIR = (0, 0, 0), (PAIRS - 1, (PAIRS - 1) // 2, (PAIRS - 1) % 2)

        def after(pair):
            if pair is None:
                return FIRST_PAIR
            n, half, u = pair
            return n + 1, half + u, 1 - u

        def pair_loop(eng, body):
            body(FIRST_PAIR, PLAN_FIRST, True, False)
            with eng.Fori(0, PAIRS // 2 - 1) as it:
                body((2 * it + 1, it, 1), PLAN, False, False)
                body((2 * it + 2, it + 1, 0), PLAN, False, False)
            body(LAST_PAIR, PLAN_LAST, False, True)

        def turns_before(b):
            return 0 if isinstance(b, int) and b == 0 else 8 * b - 4

        def add_tile(eng, n, s, g):
            qb, kt = s // KT, s % KT
            a = acc[g][qb % 2][:, :]
            eng.wait_ge(p_made[g], 1 + STEPS * n + s + 1)
            eng.wait_ge(sum_done[g], CREDIT + (KT - 1) * (QB * n + qb) + kt - 1)
            so_far = prob[g][(s - 1) % RING][:, :] if kt == 1 else a
            eng.tensor_tensor(a, so_far, prob[g][s % RING][:, :], ALU.add).then_inc(sum_done[g], 1)

        W1_ACT = 3

        def load_pair_weights(eng, n, u):
            c = n * P
            eng.dma_start(wqp[u][:, :, :], wq[:, bass.ds(c, P)].rearrange("(c p) n -> p c n", p=P)).then_inc(w_loaded[u], 16)
            eng.dma_start(wkp0[u][:, :], wkv[0:P, bass.ds(c, P)]).then_inc(w_loaded[u], 16)
            eng.dma_start(wkp1[u][0:CDIM - P, :], wkv[P:CDIM, bass.ds(c, P)]).then_inc(w_loaded[u], 16)

        @block.sync
        def _(sp):
            sp.wait_ge(clear_ctx, 2)
            sp.dma_start(mask8[0:NULL_TILE, :], mask[0, 0:NULL_TILE * P].rearrange("(t p) -> t p", p=P)).then_inc(ld_mask, 16)
            sp.dma_start(mask8[NULL_TILE:KT, 0:NULL_ROW], mask[:, NULL_TILE * P:CTX]).then_inc(ld_mask, 16)
            sp.dma_start(ctxA[:, 0:NULL_TILE, 0:CDIM], ctx_in[0, 0:NULL_TILE * P, :].rearrange("(t p) c -> p t c", p=P)).then_inc(ld_ctx, 16)
            sp.dma_start(ctxA[0:NULL_ROW, NULL_TILE, 0:CDIM], ctx_in[0, NULL_TILE * P:CTX, :]).then_inc(ld_ctx, 16)
            sp.dma_start(grow[:, :], g_norm.rearrange("(c p) -> c p", p=P)).then_inc(ld_gn, 16)
            for c in range(4):
                if c == 1:
                    load_pair_weights(sp, 0, 0)
                sp.dma_start(xs[:, 4 * c:4 * c + 4, :], x[0, c * QW:(c + 1) * QW, :].rearrange("(t p) d -> p t d", p=P)).then_inc(ld_x[c], 16)
            sp.dma_start(wv0[:, :], wkv[0:P, INNER:2 * INNER]).then_inc(ld_wv, 16)
            sp.dma_start(wv1[0:CDIM - P, :], wkv[P:CDIM, INNER:2 * INNER]).then_inc(ld_wv, 16)
            sp.wait_ge(init, 4)
            row = CDIM - P
            sp.dma_start(wv1[row + 1:row + 2, :].rearrange("a (h d) -> a h d", h=HEADS),
                         null_kv[1:2, :].unsqueeze(1).broadcast_to([1, HEADS, HD])).then_inc(ld_null, 16)
            for u in range(2):
                sp.dma_start(wkp1[u][row:row + 1, :].rearrange("a (h d) -> a h d", h=2),
                             null_kv[0:1, :].unsqueeze(1).broadcast_to([1, 2, HD])).then_inc(ld_null, 16)
            for c, s in enumerate((s0, s1, s2)):
                sp.dma_start(scol[:, c:c + 1], s.unsqueeze(0).broadcast_to([P, 1])).then_inc(ld_g, 16)

            def store_v(kt):
                sp.wait_ge(vh_free, 2 * (kt + 1))
                sp.dma_start(v_dram[:, :, kt, :].rearrange("r p d -> p r d"),
                             vsb[kt % 2][:, :].rearrange("p (r d) -> p r d", d=P)).then_inc(v_stored[kt % 2], 16)

            def copy_k(n, u):
                sp.wait_ge(k_hi, 8 * n + 8)
                for g in range(2):
                    sp.dma_start(krest[u][g][hi_rows(g), :].bitcast(F32), khl[u][g][hi_rows(g), :].bitcast(F32)).then_inc(k_copied, 16)

            def copy_q(n, u, cols, chunks, copied):
                sp.wait_ge(q_hi, 8 * n + 2 * chunks)
                for g in range(2):
                    sp.dma_start(qdup[u][g][lo_rows(g), cols].bitcast(F32), qdup[u][g][hi_rows(g), cols].bitcast(F32)).then_inc(copied, 16)

            def set_shift(n, u, g):
                sp.wait_ge(row_made[g], n + 1)
                r = shift_row(g)
                sp.dma_start(qrest[u][g][r:r + 1, :].bitcast(F32),
                             rowbuf[g][:, :].bitcast(F32)).then_inc(shift_set, 16)

            for _, job in HEAD:
                if job[0] == "V" and job[1] % 2 and job[2]:
                    store_v(job[1] // 2)
                    if job[1] == 2 * KT - 1:
                        for r in range(2):
                            sp.wait_ge(v_stored[r], 16 * ((KT + 1 - r) // 2))
                        sp.dma_start(vp[0][:, :, :], v_dram[0]).then_inc(v_loaded, 16)
                elif job == ("K", 3):
                    copy_k(0, 0)
                elif job[0] == "Q":
                    copy_q(0, 0, slice(job[1] * QW, (job[1] + 1) * QW), job[1] + 1, q0_copied[job[1]])
                elif job == ("MX", 0):
                    sp.wait_ge(init, 11)
                    set_shift(0, 0, 0)
                elif job[0] == "MX":
                    set_shift(0, 0, 1)

            def load_ot(b):
                sp.dma_start(otb[:, :, :], o_dram[:, :, bass.ds(b * QW, QW)].rearrange("k p q -> p k q")).then_inc(ot_loaded, 16)

            def body(pair, plan, first, last):
                n, half, u = pair
                nn, nhalf, nu = after(pair)

                def store_o(n, qb):
                    sp.wait_ge(norm_done, 2 + 4 * n + qb + 1)
                    sp.dma_start(o_dram[n, :, qb * QW:(qb + 1) * QW], onorm[qb % 2][:, :]).then_inc(o_stored[qb % 2], 16)

                if not last:
                    if not first:
                        sp.wait_ge(q_lo, 8 * n)
                    load_pair_weights(sp, nn, nu)
                    copy_k(nn, nu)
                    if not first:
                        store_o(n - 1, QB - 1)
                        sp.wait_ge(pv_done, CREDIT + STEPS * n)
                    sp.dma_start(vp[nu][:, :, :], v_dram[nn]).then_inc(v_loaded, 16)
                    copy_q(nn, nu, slice(0, SEQ), 4, q_copied)
                else:
                    store_o(n - 1, QB - 1)
                    sp.wait_ge(pv_done, CREDIT + STEPS * n)
                    sp.dma_start(k0raw[:, :, :], k0.rearrange("(c p) n -> p c n", p=P)).then_inc(ld_raw, 16)
                    sp.dma_start(k2raw[:, :, :], k2.rearrange("(c p) n -> p c n", p=P)).then_inc(ld_raw, 16)
                    sp.dma_start(k1raw[:, :, :], k1.rearrange("(c p) n -> p c n", p=P)).then_inc(ld_raw, 16)
                    sp.dma_start(wo_sb[:, :, :], wout.rearrange("(c p) n -> p c n", p=P)).then_inc(ld_tail, 16)
                    sp.dma_start(xres[:, :, :], x[0].rearrange("(t p) d -> p t d", p=P)).then_inc(ld_tail, 16)
                    sp.dma_start(gout[:, :], g_out.unsqueeze(0).broadcast_to([P, DIM])).then_inc(ld_tail, 16)
                store_o(n, 0)
                if not last:
                    if first:
                        sp.wait_ge(init, 17)
                    set_shift(nn, nu, 0)
                store_o(n, 1)
                if last:
                    sp.wait_ge(o_stored[0], 16 * 2 * PAIRS)
                    load_ot(0)
                store_o(n, 2)
                if not last:
                    set_shift(nn, nu, 1)
                else:
                    store_o(n, 3)

            pair_loop(sp, body)

            def store_out(b):
                for t in range(4):
                    sp.wait_ge(res_made, 4 * b + t + 1)
                    sp.dma_start(out[0, bass.ds(b * QW + t * P, P), :], obuf[t % 2][:, :]).then_inc(out_stored[t % 2], 16)

            sp.wait_ge(o_stored[1], 16 * 2 * PAIRS)
            sp.wait_ge(c_made, 4)
            load_ot(1)
            for r in range(2):
                sp.wait_ge(o_stored[r], 16 * (1 + 2 * PAIRS))
            with sp.Fori(0, QB - 2) as b:
                sp.wait_ge(c_made, 4 * b + 8)
                load_ot(b + 2)
                store_out(b)
            store_out(QB - 2)
            store_out(QB - 1)
            for r in range(2):
                sp.wait_ge(out_stored[r], 16 * (1 + 2 * QB))

        @block.gpsimd
        def _(gp):
            gp.memset(ctxA[:, NULL_TILE, :], 0.0).then_inc(clear_ctx, 1)
            gp.memset(mask8[:, :], 0).then_inc(clear_ctx, 1)
            gp.memset(ident[:, :], 0.0).then_inc(ident_made, 1)
            gp.wait_ge(ident_made, 1)
            gp.affine_select(out=ident[:, :], in_=ident[:, :], compare_op=ALU.not_equal, fill=1.0, base=0,
                             pattern=[[-1, P]], channel_multiplier=1).then_inc(ident_made, 1)
            gp.memset(ones[:, :], 1.0).then_inc(init, 1)
            gp.wait_ge(init, 1)
            gp.wait_ge(ident_made, 2)
            gp.wait_ge(clear_ctx, 2)
            gp.memset(wv1[CDIM - P:C1, :], 0.0).then_inc(init, 1)
            for u in range(2):
                gp.memset(wkp1[u][CDIM - P:C1, :], 0.0).then_inc(init, 1)
            gp.wait_ge(init, 4)
            gp.memset(epscol[:, :], EPS)
            gp.memset(eps2col[:, :], EPS * EPS).then_inc(init, 1)
            gp.memset(ctxA[:, 0:NULL_TILE, CDIM + 1:CAUG], 0.0).then_inc(null_set, 1)
            gp.wait_ge(clear_ctx, 1)
            gp.affine_select(out=ctxA[:, NULL_TILE, CDIM + 1:CAUG], in_=ctxA[:, NULL_TILE, CDIM + 1:CAUG],
                             compare_op=ALU.not_equal, fill=1.0, base=-NULL_ROW, pattern=[[0, 1]],
                             channel_multiplier=1).then_inc(null_set, 1)

            def clear_operands(u):
                gp.wait_ge(init, 5 + 6 * u)
                gp.wait_ge(null_set, 2)
                for g in range(2):
                    gp.wait_ge(init, 5 + 6 * u + 2 * g)
                    gp.memset(qrest[u][g][lo_rows(g), :].bitcast(F32), 0.0).then_inc(init, 1)
                    gp.memset(krest[u][g][lo_rows(g), :].bitcast(F32), 0.0).then_inc(init, 1)
                gp.wait_ge(init, 9 + 6 * u)
                for g in range(2):
                    gp.wait_ge(init, 9 + 6 * u + g)
                    r = shift_row(g)
                    gp.memset(krest[u][g][r:r + 1, :].bitcast(F32), 1.0).then_inc(init, 1)

            clear_operands(0)
            for r in range(2):
                gp.wait_ge(v_stored[r], 16 * ((KT + 1 - r) // 2))
            gp.wait_ge(tr_free, CT_N + XT_N)
            gp.wait_ge(vh_free, 2 * KT)
            gp.wait_ge(keybias_made, 2)
            clear_operands(1)
            gp.wait_ge(init, 17)

            def body(pair, plan, first, last):
                n, half, u = pair

                def normalise(n, qb):
                    gp.wait_ge(rec_made, 4 * n + qb + 1)
                    gp.wait_ge(o_copied, 2 + 4 * n + qb + 1)
                    gp.wait_ge(o_stored[qb % 2], 16 * (1 + 2 * n + qb // 2))
                    gp.tensor_tensor(onorm[qb % 2][:, :], oraw[qb % 2][:, :], rec[qb % 2][:, :],
                                     ALU.mult).then_inc(norm_done, 1)

                for s in range(STEPS):
                    for g in range(2):
                        if s % KT and gpsimd_sums(g, s, last):
                            add_tile(gp, n, s, g)
                    if s == L_STEPS[0] - KT + 2 and not first:
                        normalise(n - 1, QB - 1)
                    for qb, step in L_STEPS.items():
                        if s == step + 2:
                            normalise(n, qb)
                if last:
                    normalise(n, QB - 1)

            gp.sem_inc(norm_done, 2)
            gp.sem_inc(o_stored[0], 16)
            gp.sem_inc(o_stored[1], 16)
            gp.sem_inc(sum_done[0], CREDIT)
            pair_loop(gp, body)

            gp.wait_ge(ld_raw, 48)
            gp.wait_ge(pv_done, CREDIT + STEPS * PAIRS)
            for k in range(W1_ACT, FK):
                gp.tensor_scalar(w1[:, k, :], k1raw[:, k, :], 2.0, -1.0, ALU.mult, ALU.add).then_inc(w1_made[1], 1)

        @block.scalar
        def _(act):
            act.sem_inc(o_copied, 2)
            act.sem_inc(p_made[0], 1)
            act.sem_inc(p_made[1], 1)
            act.sem_inc(f_free, 3)

            def wait_side(j, pair):
                slot, before = slot_of(j, pair)
                act.wait_ge(side_made[slot], before + 1)
                return slot

            def side(j, job, pair):
                nxt, _, nu = after(pair)
                if job[0] == "K":
                    if job[1] == 0 and pair is not None:
                        for r in range(2):
                            act.wait_ge(v_stored[r], 16 * ((KT + 1 - r) // 2))
                        act.wait_ge(keybias_made, 2)
                    slot = wait_side(j, pair)
                    cols = slice(job[1] * KCH, (job[1] + 1) * KCH)
                    for g in range(2):
                        act.activation(khl[nu][g][hi_rows(g), cols], ps_side[slot][hi_rows(g), 0, 0:KCH],
                                       ACT.Copy).then_inc(k_hi, 1)
                elif job[0] == "Q":
                    slot = wait_side(j, pair)
                    cols = slice(job[1] * QW, (job[1] + 1) * QW)
                    for g in range(2):
                        act.activation(qdup[nu][g][hi_rows(g), cols], ps_side[slot][hi_rows(g), 0, :],
                                       ACT.Copy).then_inc(q_hi, 1)
                elif job[0] == "MX":
                    slot = wait_side(j, pair)
                    g = job[1]
                    act.wait_ge(shift_set, 32 * nxt)
                    act.activation(rowbuf[g][:, :], ps_side[slot][0:QT, 0, 0:P], ACT.Copy,
                                   scale=-1.0).then_inc(row_made[g], 1)
                    act.wait_ge(row_made[g], nxt + 1)
                    act.sem_inc(side_free[slot], 1)

            def evac_v(h):
                kt, half = h // 2, h % 2
                act.wait_ge(vh_made, h + 1)
                if half == 0 and kt >= 2:
                    act.wait_ge(v_stored[kt % 2], 16 * (kt // 2))
                act.activation(vsb[kt % 2][:, half * 512:(half + 1) * 512], ps_o[h % 2][:, :],
                               ACT.Copy).then_inc(vh_free, 1)

            roots = iter(range(4))

            def root():
                c = next(roots)
                act.wait_ge(ln_var, c + 1)
                act.activation(sd[:, 4 * c:4 * c + 4], mv[:, 4 * c:4 * c + 4, 1], ACT.Sqrt, scale=1.0 + EPS,
                               bias=eps2col[:, :]).then_inc(ln_sd, 1)

            act.wait_ge(init, 5)
            for n, job in HEAD:
                if job[0] == "CT":
                    i = job[1]
                    tiles = min(2, KT - 2 * i)
                    cols = slice(2 * i * P, (2 * i + tiles) * P)
                    act.wait_ge(tr_made, i + 1)
                    act.activation(cT0[:, cols], ps_s[i % 2][:, 0:tiles * P], ACT.Copy)
                    act.activation(cT1[:, cols], ps_s[i % 2][0:C1, 2 * P:(2 + tiles) * P], ACT.Copy).then_inc(tr_free, 1)
                    if i >= CT_N - 2:
                        root()
                elif job[0] == "XT":
                    t = 2 * job[1]
                    i = CT_N + job[1]
                    act.wait_ge(tr_made, i + 1)
                    for c in range(DC):
                        copied = act.activation(xT[:, c, t * P:(t + 2) * P], ps_s[i % 2][:, c * 2 * P:(c + 1) * 2 * P],
                                                ACT.Copy, scale=gcol[:, c:c + 1])
                    copied.then_inc(tr_free, 1)
                elif job[0] == "V":
                    if job[2]:
                        evac_v(job[1])
                else:
                    side(n, job, None)
                    if job in (("K", 1), ("K", 2)):
                        root()
                    if job == ("K", 3):
                        act.wait_ge(gcol_made, 1)

            def body(pair, plan, first, last):
                n, half, u = pair

                def copy_o(n, qb):
                    act.wait_ge(pv_done, CREDIT + STEPS * n + KT * (qb + 1))
                    act.wait_ge(norm_done, 4 * n + qb + 1)
                    act.activation(oraw[qb % 2][:, :], ps_o[qb % 2][:, :], ACT.Copy).then_inc(o_copied, 1)

                for s in range(STEPS):
                    kt = s % KT
                    freed = consumed(s - RING) + CREDIT if s >= RING else consumed(STEPS + s - RING) + CREDIT - (KT - 1) * QB
                    for g in range(2):
                        act.wait_ge(s_made[g], STEPS * n + s + 1)
                        act.wait_ge(pv_done, STEPS * n + s + 1)
                        act.wait_ge(sum_done[g], (KT - 1) * QB * n + freed)
                        act.activation(prob[g][s % RING][:, :], ps_s[g][:, :], ACT.Exp,
                                       bias=keybias[:, kt:kt + 1], scale=SCALE).then_inc(p_made[g], 1)
                    for j, job in plan[s]:
                        side(j, job, pair)
                    if kt == 0 and s:
                        copy_o(n, s // KT - 1)
                    if s == 0 and not first:
                        copy_o(n - 1, QB - 1)
                if last:
                    copy_o(n, QB - 1)

            act.wait_ge(keybias_made, 2)
            pair_loop(act, body)

            act.wait_ge(ld_raw, 48)
            act.wait_ge(pv_done, CREDIT + STEPS * PAIRS)
            for k in range(W1_ACT):
                act.activation(w1[:, k, :], k1raw[:, k, :], ACT.Copy, scale=2.0, bias=-1.0).then_inc(w1_made[0], 1)

            def sqrt(i, r, n):
                act.wait_ge(cv_made, n + 1)
                act.activation(csd[i % 2][:, r:r + 1], cmv[i % 2][:, r, 1:2], ACT.Sqrt, bias=epscol[:, :]).then_inc(csd_made, 1)

            def chain(b, k):
                if k < 4:
                    sqrt(k, 0, 8 * b + SQ[("A", k)])
                if 1 <= k < 5:
                    sqrt(k - 1, 1, 8 * b + SQ[("B", k - 1)])
                if 4 <= k < 8:
                    t = k - 4
                    act.wait_ge(t_made, turns_before(b) + t + 1)
                    act.activation(yhi[:, :, t * P:(t + 1) * P], ps_t[t % 2][:, 0:DIM].rearrange("p (c q) -> p c q", c=DC),
                                   ACT.Copy).then_inc(yhi_made, 1)

            for k in range(8):
                chain(0, k)

            def relu(b, j, scale):
                act.wait_ge(f_made, 18 * b + j + 1)
                act.wait_ge(h_free, 16 * b + j + 1)
                act.activation(hf[j % 2][:, :], ps_f[j % 3], ACT.Relu, scale=scale).then_inc(h_made, 1)
                act.wait_ge(h_made, 16 * b + j + 1)
                act.sem_inc(f_free, 1)

            def tail(b, with_next):
                for m in range(8):
                    relu(b, m, scol[:, 0:1])
                for m in range(8):
                    if with_next:
                        chain(b + 1, m)
                    relu(b, 8 + m, scol[:, 1:2])
                for m in range(DC):
                    j = 16 + m
                    act.wait_ge(f_made, 18 * b + j + 1)
                    act.activation(fT[m][:, :], ps_f[j % 3], ACT.Copy, scale=s2x8[:, :]).then_inc(fT_made, 1)
                    act.wait_ge(fT_made, DC * b + m + 1)
                    act.sem_inc(f_free, 1)

            act.wait_ge(ld_g, 48)
            act.wait_ge(s2_made, 1)
            with act.Fori(0, QB - 1) as b:
                tail(b, True)
            tail(QB - 1, False)

        @block.vector
        def _(dve):
            dve.sem_inc(sum_done[1], CREDIT)
            dve.sem_inc(c_free, 2)
            dve.sem_inc(out_stored[0], 16)
            dve.sem_inc(out_stored[1], 16)
            dve.sem_inc(t_free, 2)
            dve.sem_inc(h_free, 2)
            dve.wait_ge(ld_mask, 32)
            dve.tensor_copy(maskf[:, :], mask8[:, :]).then_inc(maskf_made, 1)
            dve.wait_ge(maskT_made, 1)
            dve.tensor_copy(m13[:, :], ps_o[0][:, 0:KT]).then_inc(m13_made, 1)
            dve.wait_ge(m13_made, 1)
            dve.wait_ge(null_set, 2)
            dve.tensor_scalar(ctxA[:, :, CDIM], m13[:, :], -1.0, 1.0, ALU.mult, ALU.add).then_inc(flag_made, 1)
            dve.tensor_tensor(keybias[:, :], m13[:, :], ctxA[:, :, CDIM + 1], ALU.add).then_inc(keybias_made, 1)
            dve.wait_ge(keybias_made, 1)
            dve.tensor_scalar(keybias[:, :], keybias[:, :], -1.0, -MASKED, ALU.add, ALU.mult).then_inc(keybias_made, 1)

            dve.wait_ge(gT_made, 1)
            dve.tensor_copy(gcol[:, :], ps_o[1][:, 0:DC]).then_inc(gcol_made, 1)

            dve.wait_ge(ld_ctx, 32)
            for i in range(CT_N):
                for kt in range(2 * i, min(2 * i + 2, KT)):
                    masked = dve.tensor_scalar(ctxA[:, kt, 0:CDIM], ctxA[:, kt, 0:CDIM], m13[:, kt:kt + 1], None, ALU.mult)
                masked.then_inc(ctx_masked, 1)

            def statistics(c):
                dve.wait_ge(ld_x[c], 16)
                for t in range(4 * c, 4 * c + 4):
                    dve.bn_stats(st[:, t, :], xs[:, t, :]).then_inc(ln_stats, 1)
                dve.wait_ge(ln_stats, 4 * (c + 1))
                for t in range(4 * c, 4 * c + 4):
                    got = dve.bn_aggr(mv[:, t, :], st[:, t, :])
                got.then_inc(ln_var, 1)

            def normalise(c):
                dve.wait_ge(ln_sd, c + 1)
                dve.reciprocal(rs[:, 4 * c:4 * c + 4], sd[:, 4 * c:4 * c + 4]).then_inc(ln_rs, 1)
                dve.wait_ge(ln_rs, c + 1)
                dve.wait_ge(ln_var, c + 1)
                for t in range(4 * c, 4 * c + 4):
                    dve.tensor_scalar(xs[:, t, :], xs[:, t, :], mv[:, t, 0:1], rs[:, t:t + 1],
                                      ALU.subtract, ALU.mult).then_inc(ln_out, 1)

            def side(j, job, pair):
                nxt, _, nu = after(pair)
                slot, before = slot_of(j, pair)
                if job[0] in "KQ":
                    c = job[1]
                    if job[0] == "K":
                        w, hi, whole, rest, lo_done = KCH, khl, k_hi, khl, k_lo
                    else:
                        w, hi, whole, rest, lo_done = QW, qdup, q_hi, qrest, q_lo
                    cols = slice(c * w, (c + 1) * w)
                    for g in range(2):
                        dve.wait_ge(whole, 8 * nxt + 2 * c + g + 1)
                        rows = lo_rows(g) if job[0] == "K" else hi_rows(g)
                        last = dve.tensor_tensor(rest[nu][g][rows, cols], ps_side[slot][hi_rows(g), 0, 0:w],
                                                 hi[nu][g][hi_rows(g), cols].bitcast(F32), ALU.subtract)
                        last.then_inc(lo_done, 1)
                    dve.wait_ge(lo_done, 8 * nxt + 2 * c + 2)
                    dve.sem_inc(side_free[slot], 1)
                elif job[0] == "SA":
                    _, g, qt, half = job
                    dve.wait_ge(side_made[slot], before + 1)
                    dve.reduce_max(mxh[:, g, qt, half:half + 1], ps_side[slot][:, :, 0:MXW], AX.XY).then_inc(side_free[slot], 1)
                    if (qt, half) == (QT - 1, 1):
                        dve.wait_ge(side_free[slot], before + 1)
                        dve.reduce_max(mx[:, g, :], mxh[:, g, :, :], AX.X).then_inc(mx_made, 1)
                elif job[0] in ("L", "LP"):
                    qb = job[1]
                    block = 4 * (pair[0] - 1 if job[0] == "LP" else pair[0]) + qb
                    dve.wait_ge(side_made[slot], before + 1)
                    dve.wait_ge(norm_done, block + 1)
                    dve.reciprocal(rec[qb % 2][:, :], ps_side[slot][:, 0, :]).then_inc(rec_made, 1)
                    dve.wait_ge(rec_made, block + 1)
                    dve.sem_inc(side_free[slot], 1)

            statistics(0)
            statistics(1)
            normalise(0)
            normalise(1)
            beside_k = {0: lambda: statistics(2), 1: lambda: statistics(3), 2: lambda: normalise(2), 3: lambda: normalise(3)}
            for j, job in HEAD:
                if j is not None:
                    side(j, job, None)
                    if job[0] == "K":
                        beside_k[job[1]]()

            def body(pair, plan, first, last):
                n, half, u = pair
                for s in range(STEPS):
                    for j, job in plan[s]:
                        side(j, job, pair)
                    if s % KT and not gpsimd_sums(1, s, last):
                        add_tile(dve, n, s, 1)
                    if last and s == 20:
                        dve.wait_ge(ld_raw, 48)
                        dve.wait_ge(ld_g, 48)
                        dve.tensor_tensor(w0[:, :, :], k0raw[:, 0:DC, :], k0raw[:, DC:2 * DC, :], ALU.subtract).then_inc(w_small_made, 1)
                        dve.tensor_scalar(w2[:, :, :], k2raw[:, :, :], 2.0, -1.0, ALU.mult, ALU.add).then_inc(w_small_made, 1)
                        dve.tensor_scalar(s2x8[:, :], scol[:, 2:3], 8.0, None, ALU.mult).then_inc(s2_made, 1)

            pair_loop(dve, body)

            def chain(b, k):
                base = CHAIN_N * b

                def step(instruction, key):
                    instruction.then_inc(cstep, 1)
                    dve.wait_ge(cstep, base + ORDER[key])

                if k < 4:
                    i = k
                    dve.wait_ge(c_made, 4 * b + i + 1)
                    step(dve.bn_stats(cst[i % 2][:, 0, :], ps_c[i % 2][:, 0:DIM]), ("A1", i))
                    dve.sem_inc(stood, 1)
                    dve.bn_aggr(cmv[i % 2][:, 0, :], cst[i % 2][:, 0, :]).then_inc(cv_made, 1)
                if 1 <= k < 5:
                    i = k - 1
                    dve.wait_ge(csd_made, 8 * b + SQ[("A", i)] + 1)
                    step(dve.reciprocal(crs[i % 2][:, 0:1], csd[i % 2][:, 0:1]), ("B1", i))
                    dve.tensor_scalar(attn[i % 2][:, :], ps_c[i % 2][:, 0:DIM], cmv[i % 2][:, 0, 0:1], crs[i % 2][:, 0:1],
                                      ALU.subtract, ALU.mult).then_inc(c_free, 1)
                    dve.wait_ge(c_free, 2 + 4 * b + i + 1)
                    step(dve.tensor_tensor(attn[i % 2][:, :], attn[i % 2][:, :], gout[:, :], ALU.mult), ("B2", i))
                    xr = xres[:, bass.ds(4 * b + i, 1), :].rearrange("p a d -> p (a d)")
                    step(dve.tensor_tensor(xr, xr, attn[i % 2][:, :], ALU.add), ("B3", i))
                    dve.sem_inc(stood, 1)
                    step(dve.bn_stats(cst[i % 2][:, 1, :], xr), ("B4", i))
                    dve.sem_inc(stood, 1)
                    dve.bn_aggr(cmv[i % 2][:, 1, :], cst[i % 2][:, 1, :]).then_inc(cv_made, 1)
                if 2 <= k < 6:
                    i = k - 2
                    dve.wait_ge(csd_made, 8 * b + SQ[("B", i)] + 1)
                    step(dve.reciprocal(crs[i % 2][:, 1:2], csd[i % 2][:, 1:2]), ("C1", i))
                    xr = xres[:, bass.ds(4 * b + i, 1), :].rearrange("p a d -> p (a d)")
                    if i >= 2:
                        dve.wait_ge(t_made, turns_before(b) + i - 1)
                    dve.tensor_scalar(ysb[i % 2][:, :], xr, cmv[i % 2][:, 1, 0:1], crs[i % 2][:, 1:2],
                                      ALU.subtract, ALU.mult).then_inc(y_made, 1)
                if 4 <= k < 8:
                    t = k - 4
                    dve.wait_ge(yhi_made, 4 * b + t + 1)
                    dve.tensor_tensor(ylo[:, :, t * P:(t + 1) * P], ps_t[t % 2][:, 0:DIM].rearrange("p (c q) -> p c q", c=DC),
                                      yhi[:, :, t * P:(t + 1) * P].bitcast(F32), ALU.subtract).then_inc(y_split, 1)
                    dve.wait_ge(y_split, 4 * b + t + 1)
                    dve.sem_inc(t_free, 1)

            dve.wait_ge(pv_done, CREDIT + STEPS * PAIRS)
            dve.wait_ge(ld_tail, 48)
            chain(0, 0)
            side(*PLAN_LAST[STEPS][0], LAST_PAIR)
            for k in range(1, 8):
                chain(0, k)

            def split(b, j):
                hi, lo = (h0hi, h0lo) if j < 8 else (h1hi, h1lo)
                dve.wait_ge(h_made, 16 * b + j + 1)
                dve.tensor_copy(hi[:, j % 8, :], hf[j % 2][:, :]).then_inc(split_step, 1)
                dve.wait_ge(split_step, 16 * b + j + 1)
                dve.tensor_tensor(lo[:, j % 8, :], hf[j % 2][:, :], hi[:, j % 8, :].bitcast(F32),
                                  ALU.subtract).then_inc(h_free, 1)

            def tail(b, with_next):
                for j in range(8):
                    split(b, j)
                for j in range(8):
                    if with_next:
                        chain(b + 1, j)
                    split(b, 8 + j)
                for t in range(4):
                    dve.wait_ge(t_made, 8 * b + (8 if with_next else 4) + t + 1)
                    dve.wait_ge(out_stored[t % 2], 16 * (1 + 2 * b + t // 2))
                    xr = xres[:, bass.ds(4 * b + t, 1), :].rearrange("p a d -> p (a d)")
                    dve.tensor_tensor(obuf[t % 2][:, :], ps_t[t % 2][:, 0:DIM], xr, ALU.add).then_inc(res_made, 1)
                    dve.wait_ge(res_made, 4 * b + t + 1)
                    dve.sem_inc(t_free, 1)

            with dve.Fori(0, QB - 1) as b:
                tail(b, True)
            tail(QB - 1, False)

        @block.tensor
        def _(pe):
            pe.sem_inc(pv_done, CREDIT)

            pe.wait_ge(maskf_made, 1)
            pe.wait_ge(ident_made, 2)
            pe.transpose(ps_o[0][:, 0:KT], maskf[:, :], ident[0:KT, 0:KT]).then_inc(maskT_made, 1)
            pe.wait_ge(ld_gn, 16)
            pe.transpose(ps_o[1][:, 0:DC], grow[:, :], ident[0:DC, 0:DC]).then_inc(gT_made, 1)
            def project_v(h, part):
                kt, half = h // 2, h % 2
                keys, cols = slice(kt * P, (kt + 1) * P), slice(half * 512, (half + 1) * 512)
                if part == 0:
                    if h == 0:
                        pe.wait_ge(ld_wv, 32)
                    if h < 2:
                        pe.wait_ge(m13_made, 1)
                        pe.wait_ge(gcol_made, 1)
                    else:
                        pe.wait_ge(vh_free, h - 1)
                    pe.matmul(ps_o[h % 2][:, :], cT0[:, keys], wv0[:, cols], start=True, stop=False)
                else:
                    pe.matmul(ps_o[h % 2][:, :], cT1[:, keys], wv1[:, cols], start=False, stop=True).then_inc(vh_made, 1)

            def side(j, job, pair):
                nxt, nhalf, nu = after(pair)
                slot, before = slot_of(j, pair)
                if not (pair is None and before == 0):
                    pe.wait_ge(side_free[slot], before)
                ps = ps_side[slot]
                if job[0] == "K":
                    if job[1] == 0:
                        pe.wait_ge(w_loaded[nu], 48 * (nhalf + 1))
                    cols = slice(job[1] * KCH, (job[1] + 1) * KCH)
                    pe.matmul(ps[:, 0, 0:KCH], wkp0[nu][:, :], cT0[:, cols], start=True, stop=False)
                    pe.matmul(ps[:, 0, 0:KCH], wkp1[nu][:, :], cT1[:, cols], start=False, stop=True).then_inc(side_made[slot], 1)
                elif job[0] == "Q":
                    if pair is None:
                        pe.wait_ge(tr_free, CT_N + 2 * job[1] + 2)
                    cols = slice(job[1] * QW, (job[1] + 1) * QW)
                    for c in range(DC):
                        last = pe.matmul(ps[:, 0, :], wqp[nu][:, c, :], xT[:, c, cols], start=(c == 0), stop=(c == DC - 1))
                    last.then_inc(side_made[slot], 1)
                elif job[0] == "SA":
                    _, g, qt, half = job
                    if pair is None and qt % 4 == 0 and half == 0:
                        pe.wait_ge(q0_copied[qt // 4], 32)
                    elif (g, qt, half) == (0, 0, 0):
                        pe.wait_ge(q_copied, 32 * nxt)
                    if (g, qt, half) == (0, 0, 0):
                        pe.wait_ge(k_lo, 8 * (nxt + 1))
                    for j in range(2):
                        cols = slice(half * MXH + j * MXW, half * MXH + (j + 1) * MXW)
                        last = pe.matmul(ps[:, j, 0:MXW], qdup[nu][g][:, qt * P:(qt + 1) * P], khl[nu][g][:, cols],
                                         start=True, stop=True)
                    last.then_inc(side_made[slot], 1)
                elif job[0] == "MX":
                    g = job[1]
                    pe.wait_ge(mx_made, 2 * nxt + g + 1)
                    pe.transpose(ps[0:QT, 0, 0:P], mx[:, g, :], ident[:, :]).then_inc(side_made[slot], 1)
                else:
                    qb = job[1]
                    block = QB * (pair[0] - 1 if job[0] == "LP" else pair[0]) + qb
                    for g in range(2):
                        pe.wait_ge(sum_done[g], CREDIT + (KT - 1) * (block + 1))
                        last = pe.matmul(ps[g * HD:(g + 1) * HD, 0, :], ones[:, :], acc[g][qb % 2][:, :], start=True, stop=True)
                    last.then_inc(side_made[slot], 1)

            for n, job in HEAD:
                if job[0] == "CT":
                    i = job[1]
                    if i == 0:
                        pe.wait_ge(flag_made, 1)
                    pe.wait_ge(ctx_masked, i + 1)
                    if i >= 2:
                        pe.wait_ge(tr_free, i - 1)
                    for k in range(min(2, KT - 2 * i)):
                        pe.transpose(ps_s[i % 2][:, k * P:(k + 1) * P], ctxA[:, 2 * i + k, 0:P], ident[:, :])
                        last = pe.transpose(ps_s[i % 2][0:C1, (2 + k) * P:(3 + k) * P], ctxA[:, 2 * i + k, P:CAUG], ident[:, :])
                    last.then_inc(tr_made, 1)
                    if i == CT_N - 1:
                        pe.wait_ge(tr_free, CT_N)
                        pe.wait_ge(ld_null, 48)
                elif job[0] == "XT":
                    t = 2 * job[1]
                    i = CT_N + job[1]
                    if t % 4 == 0:
                        pe.wait_ge(ln_out, t + 4)
                    pe.wait_ge(tr_free, i - 1)
                    for c in range(DC):
                        for k in range(2):
                            last = pe.transpose(ps_s[i % 2][:, (2 * c + k) * P:(2 * c + k + 1) * P],
                                                xs[:, t + k, c * P:(c + 1) * P], ident[:, :])
                    last.then_inc(tr_made, 1)
                elif job[0] == "V":
                    project_v(*job[1:])
                else:
                    side(n, job, None)
            pe.wait_ge(vh_free, 2 * KT)

            def values(n, u, s):
                qb, kt = s // KT, s % KT
                if kt == 0:
                    pe.wait_ge(o_copied, 4 * n + qb + 1)
                for g in range(2):
                    pe.wait_ge(p_made[g], 1 + STEPS * n + s + 1)
                    last = pe.matmul(ps_o[qb % 2][hi_rows(g), :], vp[u][:, kt, hi_rows(g)], prob[g][s % RING][:, :],
                                     start=(kt == 0), stop=(kt == KT - 1))
                last.then_inc(pv_done, 1)

            def body(pair, plan, first, last):
                n, half, u = pair
                pe.wait_ge(k_copied, 32 * (n + 1))
                pe.wait_ge(q_lo, 8 * (n + 1))
                pe.wait_ge(shift_set, 32 * (n + 1))
                if u == 0:
                    pe.wait_ge(init, 11)
                else:
                    pe.wait_ge(init, 17)

                for s in range(STEPS):
                    qb, kt = s // KT, s % KT
                    qs, ks = slice(qb * QW, (qb + 1) * QW), slice(kt * P, (kt + 1) * P)
                    for g in range(2):
                        pe.wait_ge(p_made[g], 1 + STEPS * n + s)
                        pe.matmul(ps_s[g][:, :], khl[u][g][:, ks], qdup[u][g][:, qs], start=True, stop=False)
                        pe.matmul(ps_s[g][:, :], krest[u][g][:, ks], qrest[u][g][:, qs], start=False,
                                  stop=True).then_inc(s_made[g], 1)
                    for j, job in plan[s]:
                        side(j, job, pair)
                    if s:
                        values(n, u, s - 1)
                    elif not first:
                        values(n - 1, 1 - u, STEPS - 1)
                    if s == 0:
                        pe.wait_ge(v_loaded, 16 * (n + 1))
                if last:
                    values(n, u, STEPS - 1)

            pair_loop(pe, body)

            pe.wait_ge(ld_tail, 48)

            def project_out(b, t):
                if t == 0:
                    pe.wait_ge(ot_loaded, 16 * (b + 1))
                pe.wait_ge(c_free, 4 * b + t + 1)
                for k in range(PAIRS):
                    last = pe.matmul(ps_c[t % 2][:, 0:DIM], otb[:, k, t * P:(t + 1) * P], wo_sb[:, k, :],
                                     start=(k == 0), stop=(k == PAIRS - 1))
                last.then_inc(c_made, 1)

            def turn_y(b, t):
                pe.wait_ge(y_made, 4 * b + t + 1)
                pe.wait_ge(t_free, turns_before(b) + t + 1)
                for c in range(DC):
                    last = pe.transpose(ps_t[t % 2][:, c * P:(c + 1) * P], ysb[t % 2][:, c * P:(c + 1) * P], ident[:, :])
                last.then_inc(t_made, 1)

            def chain(b, k):
                if k < 4:
                    project_out(b, k)
                else:
                    turn_y(b, k - 4)

            chain(0, 0)
            side(*PLAN_LAST[STEPS][0], LAST_PAIR)
            for k in range(1, 4):
                chain(0, k)
            pe.wait_ge(o_copied, 2 + 4 * PAIRS)
            for k in range(4, 8):
                chain(0, k)
            for r in range(2):
                pe.wait_ge(side_free[r], TOTAL_N // 2)
            pe.wait_ge(w_small_made, 2)

            def layer(b, j, weights, m, hi, lo, depth):
                pe.wait_ge(f_free, 18 * b + j + 1)
                for k in range(depth):
                    for part in (hi, lo):
                        last = pe.matmul(ps_f[j % 3], weights[:, k, m * P:(m + 1) * P], part[:, k, :],
                                         start=(k == 0 and part is hi), stop=(k == depth - 1 and part is lo))
                last.then_inc(f_made, 1)

            def tail(b, with_next):
                pe.wait_ge(y_split, 4 * b + 4)
                for m in range(8):
                    layer(b, m, w0, m, yhi, ylo, DC)
                pe.wait_ge(w1_made[0], W1_ACT)
                pe.wait_ge(w1_made[1], FK - W1_ACT)
                for m in range(8):
                    if with_next:
                        chain(b + 1, m)
                    if m == 0:
                        pe.wait_ge(h_free, 2 + 16 * b + 8)
                    layer(b, 8 + m, w1, m, h0hi, h0lo, FK)
                pe.wait_ge(h_free, 2 + 16 * b + 16)
                for m in range(DC):
                    layer(b, 16 + m, w2, m, h1hi, h1lo, FK)
                pe.wait_ge(fT_made, DC * (b + 1))
                for t in range(4):
                    pe.wait_ge(t_free, 8 * b + (8 if with_next else 4) + t + 1)
                    for c in range(DC):
                        last = pe.transpose(ps_t[t % 2][:, c * P:(c + 1) * P], fT[c][:, t * P:(t + 1) * P], ident[:, :])
                    last.then_inc(t_made, 1)

            with pe.Fori(0, QB - 1) as b:
                tail(b, True)
            tail(QB - 1, False)


_INS = ["x", "ctx_768", "mask_BxS2_bf1", "L0_xattn_g_norm", "L0_xattn_null_kv", "L0_xattn_Wq", "L0_xattn_Wkv",
        "L0_xattn_Wout", "L0_xattn_g_out", "L0_ffn_k0", "L0_ffn_k1", "L0_ffn_k2", "L0_ffn_s0", "L0_ffn_s1", "L0_ffn_s2"]


def kernel(**inputs):
    import numpy as np
    import concourse.bacc as bacc
    from concourse.bass_utils import run_bass_kernel_spmd

    nc = bacc.Bacc("TRN2", target_bir_lowering=False, num_devices=1)
    arrays, args = {}, []
    for name in _INS:
        a = np.ascontiguousarray(inputs[name])
        if a.ndim == 0:
            a = a.reshape(1)
        arrays[f"in_{name}"] = a
        args.append(nc.dram_tensor(f"in_{name}", a.shape, mybir.dt.from_np(a.dtype), kind="ExternalInput").ap())
    out = nc.dram_tensor("out", (1, SEQ, DIM), F32, kind="ExternalOutput").ap()
    xattn_ffn_kernel(nc, *args, out)
    r = run_bass_kernel_spmd(nc, [arrays], core_ids=[0])
    return r.results[0]["out"]
```

```python
from contextlib import ExitStack

import concourse.bass as bass
from concourse import mybir

F32 = mybir.dt.float32
F32R = mybir.dt.float32r
U8 = mybir.dt.uint8
ALU = mybir.AluOpType
ACT = mybir.ActivationFunctionType
AX = mybir.AxisListType

P = 128
SEQ, DIM = 2048, 256
CTX, CDIM = 1601, 192
HEADS, HD = 16, 64
INNER = HEADS * HD
PAIRS = HEADS // 2
QT = SEQ // P
QB, QW = 4, 512
DC = DIM // P
KEYS = CTX + 1
KT = (KEYS + P - 1) // P
KPAD = KT * P
NULL_TILE, NULL_ROW = CTX // P, CTX % P
CAUG = CDIM + 2
C1 = CAUG - P
KCH = KPAD // 4
MXW = 402
MXH = 2 * MXW
FF = 1024
FK = FF // P
EPS = 1e-5
SCALE = float(HD) ** -0.5
MASKED = -30000.0
STEPS = QB * KT
RING = 4
CREDIT = 4

assert STEPS % RING == 0 and 4 * MXW >= KEYS and 4 * MXW <= KPAD and KPAD % 4 == 0


L_STEPS = {qb: KT * (qb + 1) + 2 for qb in range(QB - 1)}


def plan_side(first, last):
    plan = {s: [] for s in range(STEPS + 1)}
    if not first:
        plan[LP_STEP].append(("LP", QB - 1))
    for qb, s in L_STEPS.items():
        plan[s].append(("L", qb))
    if last:
        plan[STEPS].append(("L", QB - 1))
        plan[C_STEP].append(("C", 0))
        plan[C_STEP + 2].append(("C", 1))
    else:
        for c in range(4):
            plan[c + 1].append(("Q", c))
            plan[4 + c if c else 0].append(("K", c))
        busy = [x for s in L_STEPS.values() for x in (s, s + 1)]
        steps = [s for s in range(SA_FIRST, SA_LAST + 1) if s not in busy]
        halves = 4 * QT
        for i, s in enumerate(steps):
            for j in range(i * halves // len(steps), (i + 1) * halves // len(steps)):
                plan[s].append(("SA", j // (2 * QT), j % (2 * QT) // 2, j % 2))
        plan[31].insert(0, ("MX", 0))
        plan[49].append(("MX", 1))
    n = 0
    out = {}
    for s in range(STEPS + 1):
        out[s] = []
        for job in plan[s]:
            out[s].append((n, job))
            n += 1
    return out, n


def plan_head():
    values = iter([("V", h, part) for h in range(2 * KT) for part in range(2)])
    order = [("CT", i) for i in range(CT_N)]
    for c in range(4):
        order += [("K", c)] + [next(values) for _ in range(V_BESIDE_K[c])]

    def queries(c):
        return [("XT", 2 * c), next(values), ("XT", 2 * c + 1), next(values), ("Q", c), next(values)]

    order += queries(0) + queries(1)
    n = 0
    for c in range(4):
        for g in range(2):
            for qt in range(4 * c, 4 * c + 4):
                for half in range(2):
                    if (c, g, qt, half) == (3, 1, 13, 1):
                        order.append(("MX", 0))
                    order.append(("SA", g, qt, half))
                    n += 1
                    if n % 7 in (0, 2, 4, 6):
                        order += [job for job in (next(values, None),) if job]
        if c + 2 < 4:
            order += queries(c + 2)
    order.append(("MX", 1))
    assert not list(values)
    out, n = [], 0
    for job in order:
        if job[0] in ("CT", "XT", "V"):
            out.append((None, job))
        else:
            out.append((n, job))
            n += 1
    return out, n


CT_N = (KT + 1) // 2
XT_N = QT // 2
V_BESIDE_K = [0, 2, 2, 3]
SA_FIRST, SA_LAST = 10, 47
LP_STEP = 7
C_STEP = 30
PLAN_FIRST, FIRST_N = plan_side(True, False)
PLAN, SIDE_N = plan_side(False, False)
PLAN_LAST, LAST_N = plan_side(False, True)
C_JOBS = [n for jobs in PLAN_LAST.values() for n, job in jobs if job[0] == "C"]
HEAD, HEAD_N = plan_head()
BEFORE_1 = HEAD_N + FIRST_N
TOTAL_N = BEFORE_1 + (PAIRS - 2) * SIDE_N + LAST_N
assert SIDE_N % 2 == 0 and TOTAL_N % 2 == 0


def gpsimd_sums(g, s, last):
    if last:
        return s < STEPS - 3 if g == 0 else C_STEP <= s < C_STEP + 10 and s % 2 == 0
    if g == 0:
        return True
    return s % KT in (2, 3) or s in (LP_STEP, LP_STEP + 1) or SA_FIRST <= s <= SA_LAST + 2 and s % 2 == 0


def plan_chain():
    roots, steps = [], []
    for k in range(8):
        if k < 4:
            roots.append(("A", k))
            steps.append(("A1", k))
        if 1 <= k < 5:
            roots.append(("B", k - 1))
            steps += [("B2", k - 1), ("B3", k - 1), ("B4", k - 1)]
    return {r: n for n, r in enumerate(roots)}, {s: n + 1 for n, s in enumerate(steps)}


ROOT, ORDER = plan_chain()
CHAIN_N = len(ORDER)


def hi_rows(g):
    return slice(HD * g, HD * g + HD)


def lo_rows(g):
    return slice(HD * (1 - g), HD * (1 - g) + HD)


def shift_row(g):
    return HD * (1 - g)


def consumed(s):
    return (KT - 1) * (s // KT) + max(s % KT, 1)


def xattn_ffn_kernel(nc, x, ctx_in, mask, g_norm, null_kv, wq, wkv, wout, g_out, k0, k1, k2, s0, s1, s2, out):
    v_dram = nc.dram_tensor("v_scratch", [PAIRS, P, KT, P], F32, kind="Internal").ap()
    o_dram = nc.dram_tensor("o_scratch", [PAIRS, P, SEQ], F32, kind="Internal").ap()

    with ExitStack() as es:
        def psum(name, shape):
            return es.enter_context(nc.psum_tensor(name, shape, F32))

        def sem(name):
            return es.enter_context(nc.semaphore(name))

        start = (nc.sbuf_base + 63) // 64 * 64
        at = {"": start}

        def sb(name, shape, dt=F32, region=""):
            size = 1
            for n in shape[1:]:
                size *= n
            size = (size * (1 if dt == U8 else 4) + 63) // 64 * 64
            t = nc.alloc_sbuf_tensor_at(name, shape, dt, offset=at[region])
            at[region] += size
            return t

        ident = sb("ident", [P, P])
        ones = sb("ones", [P, HD])
        epscol = sb("epscol", [P, 1])
        preload = sb("preload", [P, 2])
        minus_half = sb("minus_half", [P, 4])
        eps2col = sb("eps2col", [P, 1])
        keybias = sb("keybias", [P, KT])
        gcol = sb("gcol", [P, DC])
        scol = sb("scol", [P, 3])
        s2x8 = sb("s2x8", [P, 1])
        mxh = sb("mxh", [P, 2, QT, 2])
        mx = sb("mx", [P, 2, QT])
        rowbuf = [sb(f"rowbuf{g}", [QT, P], F32R) for g in range(2)]
        wqp = sb("wqp", [P, DC, P])
        wq_hi, wq_lo = sb("wq_hi", [P, DC, P], F32R), sb("wq_lo", [P, DC, P], F32R)
        wkp0 = [sb(f"wkp0_{u}", [P, P]) for u in range(2)]
        wkp1 = [sb(f"wkp1_{u}", [C1, P]) for u in range(2)]

        qdup, qrest, khl, krest = [[], []], [[], []], [[], []], [[], []]

        def operands(u):
            for g in range(2):
                qdup[u].append(sb(f"qdup{u}{g}", [P, SEQ], F32R))
                qrest[u].append(sb(f"qrest{u}{g}", [P, SEQ], F32R))
                khl[u].append(sb(f"khl{u}{g}", [P, KPAD], F32R))
                krest[u].append(sb(f"krest{u}{g}", [P, KPAD], F32R))

        at["tail0"] = at[""]
        operands(0)
        at["w02"] = at[""]
        x_hi = sb("x_hi", [P, DC, SEQ], F32R)
        at["head"] = at["tail1"] = at[""]
        operands(1)
        end_operands1 = at[""]
        cT0 = sb("cT0", [P, KPAD])
        cT1 = sb("cT1", [C1, KPAD])
        at["vp0"] = at[""]
        vp = [sb(f"vp{u}", [P, KT, P]) for u in range(2)]
        prob = [[sb(f"prob{g}{r}", [P, QW]) for r in range(RING)] for g in range(2)]
        acc = [[sb(f"acc{g}{r}", [P, QW]) for r in range(2)] for g in range(2)]
        x_lo = sb("x_lo", [P, DC, SEQ], F32R)
        onorm = sb("onorm", [P, QW])
        end_all = at[""]
        assert end_all <= nc.sbuf_usable_end, end_all

        xs = sb("xs", [P, QT, DIM], region="head")
        ctxA = sb("ctxA", [P, KT, CAUG], region="head")
        wv0 = sb("wv0", [P, INNER], region="head")
        wv1 = sb("wv1", [C1, INNER], region="head")
        vsb = [sb(f"vsb{r}", [P, INNER], region="head") for r in range(2)]
        mask8 = sb("mask8", [KT, P], U8, region="head")
        maskf = sb("maskf", [KT, P], region="head")
        grow = sb("grow", [DC, P], region="head")
        m13 = sb("m13", [P, KT], region="head")
        st = sb("st", [P, QT, 6], region="head")
        mv = sb("mv", [P, QT, 2], region="head")
        sd = sb("sd", [P, QT], region="head")
        rs = sb("rs", [P, QT], region="head")
        assert at["head"] <= end_operands1

        wo_sb = sb("wo_sb", [P, PAIRS, DIM], region="tail0")
        k0raw = sb("k0raw", [P, 2 * DC, FF], U8, region="tail0")
        k1raw = sb("k1raw", [P, FK, FF], U8, region="tail0")
        k2raw = sb("k2raw", [P, FK, DIM], U8, region="tail0")
        otb = sb("otb", [P, PAIRS, QW], region="tail0")
        xres = sb("xres", [P, QT, DIM], region="tail0")
        gout = sb("gout", [P, DIM], region="tail0")
        at["small"] = at["tail0"]
        end_operands0 = at["w02"]
        w0 = sb("w0", [P, DC, FF], F32R, region="w02")
        w2 = sb("w2", [P, FK, DIM], F32R, region="w02")
        assert at["w02"] <= at["tail1"]
        ysb = [sb(f"ysb{r}", [P, DIM], region="tail1") for r in range(2)]
        w1 = sb("w1", [P, FK, FF], F32R, region="tail1")
        yhi = sb("yhi", [P, DC, QW], F32R, region="tail1")
        ylo = sb("ylo", [P, DC, QW], F32R, region="tail1")
        h0hi = sb("h0hi", [P, FK, QW], F32R, region="tail1")
        h0lo = sb("h0lo", [P, FK, QW], F32R, region="tail1")
        h1hi = sb("h1hi", [P, FK, QW], F32R, region="tail1")
        h1lo = sb("h1lo", [P, FK, QW], F32R, region="tail1")
        hf = [sb(f"hf{r}", [P, QW], region="tail1") for r in range(2)]
        fT = [sb(f"fT{m}", [P, QW], region="tail1") for m in range(DC)]
        attn = [sb(f"attn{r}", [P, DIM], region="small") for r in range(2)]
        obuf = [sb(f"obuf{r}", [P, 2, DIM], region="tail1") for r in range(2)]
        cst = [sb(f"cst{r}", [P, 2, 6], region="small") for r in range(2)]
        cmv = [sb(f"cmv{r}", [P, 2, 2], region="small") for r in range(2)]
        cve = [sb(f"cve{r}", [P, 2], region="small") for r in range(2)]
        crs = [sb(f"crs{r}", [P, 2], region="small") for r in range(2)]
        y0 = sb("y0", [P, 4, DIM], region="vp0")
        y0st = sb("y0st", [P, 4, 6], region="vp0")
        y0mv = [sb(f"y0mv{r}", [P, 4, 2], region="vp0") for r in range(2)]
        y0var = [sb(f"y0var{r}", [P, 4], region="vp0") for r in range(2)]
        y0rs = [sb(f"y0rs{r}", [P, 4], region="vp0") for r in range(2)]
        assert at["tail1"] <= end_all, (at["tail1"], end_all)
        assert at["small"] <= end_operands0, (at["small"], end_operands0)

        ps_s = [psum(f"ps_s{g}", [P, 512]) for g in range(2)]
        ps_o = [psum(f"ps_o{r}", [P, 512]) for r in range(2)]
        ps_side = [psum(f"ps_side{r}", [P, 2, 512]) for r in range(2)]
        ps_c = ps_s
        ps_t = ps_o
        ps_f = [ps_side[0][:, 0, :], ps_side[0][:, 1, :], ps_side[1][:, 1, :]]

        ld_ctx = [sem(f"ld_ctx{c}") for c in range(3)]
        ld_mask, ld_x, ld_g = sem("ld_mask"), [sem(f"ld_x{c}") for c in range(4)], sem("ld_g")
        ld_wv, ld_null_k, ld_null_v = sem("ld_wv"), sem("ld_null_k"), sem("ld_null_v")
        init = sem("init")
        ld_gn, gT_made, gcol_made = sem("ld_gn"), sem("gT_made"), sem("gcol_made")
        ident_made = sem("ident_made")
        clear_ctx = sem("clear_ctx")
        null_set = sem("null_set")
        maskf_made, maskT_made, m13_made, keybias_made = sem("maskf_made"), sem("maskT_made"), sem("m13_made"), sem("keybias_made")
        flag_made = sem("flag_made")
        ctx_masked = sem("ctx_masked")
        tr_made, tr_free = sem("tr_made"), sem("tr_free")
        vh_made, vh_free = sem("vh_made"), sem("vh_free")
        v_stored = [sem(f"v_stored{r}") for r in range(2)]
        ln_stats, ln_var, ln_sd, ln_rs, ln_out = sem("ln_stats"), sem("ln_var"), sem("ln_sd"), sem("ln_rs"), sem("ln_out")
        side_made = [sem(f"side_made{r}") for r in range(2)]
        side_free = [sem(f"side_free{r}") for r in range(2)]
        w_loaded = [sem(f"w_loaded{u}") for u in range(2)]
        v_loaded = sem("v_loaded")
        k_hi, k_lo, q_hi, q_lo = sem("k_hi"), sem("k_lo"), sem("q_hi"), sem("q_lo")
        k_copied, q_copied, shift_set = sem("k_copied"), sem("q_copied"), sem("shift_set")
        q0_copied = [sem(f"q0_copied{c}") for c in range(4)]
        wq_rounded, wq_split, x_rounded = sem("wq_rounded"), sem("wq_split"), sem("x_rounded")
        mx_made, row_made = sem("mx_made"), [sem("row_made0"), sem("row_made1")]
        s_made = [sem(f"s_made{g}") for g in range(2)]
        p_made = [sem(f"p_made{g}") for g in range(2)]
        pv_done = sem("pv_done")
        sum_done = [sem(f"sum_done{g}") for g in range(2)]
        o_copied = sem("o_copied")
        rec_made = sem("rec_made")
        norm_done = sem("norm_done")
        o_stored = [sem(f"o_stored{r}") for r in range(2)]
        ld_tail, ld_raw, ot_loaded = sem("ld_tail"), sem("ld_raw"), sem("ot_loaded")
        s2_made, w_small_made, w1_made = sem("s2_made"), sem("w_small_made"), sem("w1_made")
        y0_stats, y0_var, y0_root = sem("y0_stats"), sem("y0_var"), sem("y0_root")
        y0_step, y0_made, half_made = sem("y0_step"), sem("y0_made"), sem("half_made")
        c_made, c_free = sem("c_made"), sem("c_free")
        t_made, t_free = sem("t_made"), sem("t_free")
        f_made, f_free = sem("f_made"), sem("f_free")
        h_made, h_free = sem("h_made"), sem("h_free")
        split_step = sem("split_step")
        cv_made, cve_made, crs_made = sem("cv_made"), sem("cve_made"), sem("crs_made")
        cstep = sem("cstep")
        stood = sem("stood")
        y_made, yhi_made, y_split = sem("y_made"), sem("yhi_made"), sem("y_split")
        fT_made = sem("fT_made")
        res_made = sem("res_made")
        out_stored = [sem(f"out_stored{r}") for r in range(2)]

        block = es.enter_context(nc.Block())

        def slot_of(j, pair):
            if pair is None:
                return j % 2, j // 2
            if isinstance(pair[0], int) and pair[0] == 0:
                j += HEAD_N
                return j % 2, j // 2
            j += BEFORE_1
            return j % 2, j // 2 + (pair[0] - 1) * (SIDE_N // 2)

        FIRST_PAIR, LAST_PAIR = (0, 0, 0), (PAIRS - 1, (PAIRS - 1) // 2, (PAIRS - 1) % 2)

        def after(pair):
            if pair is None:
                return FIRST_PAIR
            n, half, u = pair
            return n + 1, half + u, 1 - u

        def pair_loop(eng, body):
            body(FIRST_PAIR, PLAN_FIRST, True, False)
            with eng.Fori(0, PAIRS // 2 - 1) as it:
                body((2 * it + 1, it, 1), PLAN, False, False)
                body((2 * it + 2, it + 1, 0), PLAN, False, False)
            body(LAST_PAIR, PLAN_LAST, False, True)

        def turns_before(b):
            return 0 if isinstance(b, int) and b == 0 else 8 * b - 4

        def add_tile(eng, n, s, g):
            qb, kt = s // KT, s % KT
            a = acc[g][qb % 2][:, :]
            eng.wait_ge(p_made[g], 1 + STEPS * n + s + 1)
            eng.wait_ge(sum_done[g], CREDIT + (KT - 1) * (QB * n + qb) + kt - 1)
            so_far = prob[g][(s - 1) % RING][:, :] if kt == 1 else a
            eng.tensor_tensor(a, so_far, prob[g][s % RING][:, :], ALU.add).then_inc(sum_done[g], 1)

        def load_pair_weights(eng, n, u):
            c = n * P
            eng.dma_start(wqp[:, :, :], wq[:, bass.ds(c, P)].rearrange("(c p) n -> p c n", p=P)).then_inc(w_loaded[u], 16)
            eng.dma_start(wkp0[u][:, :], wkv[0:P, bass.ds(c, P)]).then_inc(w_loaded[u], 16)
            eng.dma_start(wkp1[u][0:CDIM - P, :], wkv[P:CDIM, bass.ds(c, P)]).then_inc(w_loaded[u], 16)

        @block.sync
        def _(sp):
            half = NULL_TILE // 2
            for h in range(2):
                tiles = slice(h * half, (h + 1) * half)
                sp.dma_start(ctxA[:, tiles, 0:CDIM], ctx_in[0, h * half * P:(h + 1) * half * P, :].rearrange("(t p) c -> p t c", p=P)).then_inc(ld_ctx[h], 16)
            sp.wait_ge(clear_ctx, 2)
            sp.dma_start(mask8[0:NULL_TILE, :], mask[0, 0:NULL_TILE * P].rearrange("(t p) -> t p", p=P)).then_inc(ld_mask, 16)
            sp.dma_start(mask8[NULL_TILE:KT, 0:NULL_ROW], mask[:, NULL_TILE * P:CTX]).then_inc(ld_mask, 16)
            sp.dma_start(ctxA[0:NULL_ROW, NULL_TILE, 0:CDIM], ctx_in[0, NULL_TILE * P:CTX, :]).then_inc(ld_ctx[2], 16)
            sp.dma_start(grow[:, :], g_norm.rearrange("(c p) -> c p", p=P)).then_inc(ld_gn, 16)

            def load_x(c):
                sp.dma_start(xs[:, 4 * c:4 * c + 4, :], x[0, c * QW:(c + 1) * QW, :].rearrange("(t p) d -> p t d", p=P)).then_inc(ld_x[c], 16)

            load_x(0)
            sp.wait_ge(init, 4)
            row = CDIM - P
            for u in range(2):
                sp.dma_start(wkp1[u][row:row + 1, :].rearrange("a (h d) -> a h d", h=2),
                             null_kv[0:1, :].unsqueeze(1).broadcast_to([1, 2, HD])).then_inc(ld_null_k, 16)
            load_pair_weights(sp, 0, 0)
            load_x(1)
            sp.dma_start(wv1[row + 1:row + 2, :].rearrange("a (h d) -> a h d", h=HEADS),
                         null_kv[1:2, :].unsqueeze(1).broadcast_to([1, HEADS, HD])).then_inc(ld_null_v, 16)
            sp.dma_start(wv0[:, :], wkv[0:P, INNER:2 * INNER]).then_inc(ld_wv, 16)
            sp.dma_start(wv1[0:CDIM - P, :], wkv[P:CDIM, INNER:2 * INNER]).then_inc(ld_wv, 16)
            load_x(2)
            load_x(3)
            for c, s in enumerate((s0, s1, s2)):
                sp.dma_start(scol[:, c:c + 1], s.unsqueeze(0).broadcast_to([P, 1])).then_inc(ld_g, 16)

            def store_v(kt):
                sp.wait_ge(vh_free, 2 * (kt + 1))
                sp.dma_start(v_dram[:, :, kt, :].rearrange("r p d -> p r d"),
                             vsb[kt % 2][:, :].rearrange("p (r d) -> p r d", d=P)).then_inc(v_stored[kt % 2], 16)

            def copy_k(n, u):
                sp.wait_ge(k_hi, 8 * n + 8)
                for g in range(2):
                    sp.dma_start(krest[u][g][hi_rows(g), :].bitcast(F32), khl[u][g][hi_rows(g), :].bitcast(F32)).then_inc(k_copied, 16)

            def copy_q(n, u, cols, chunks, copied):
                sp.wait_ge(q_hi, 8 * n + 2 * chunks)
                for g in range(2):
                    sp.dma_start(qdup[u][g][lo_rows(g), cols].bitcast(F32), qdup[u][g][hi_rows(g), cols].bitcast(F32)).then_inc(copied, 16)

            def set_shift(n, u, g):
                sp.wait_ge(row_made[g], n + 1)
                r = shift_row(g)
                sp.dma_start(qrest[u][g][r:r + 1, :].bitcast(F32),
                             rowbuf[g][:, :].bitcast(F32)).then_inc(shift_set, 16)

            for _, job in HEAD:
                if job[0] == "V" and job[1] % 2 and job[2]:
                    store_v(job[1] // 2)
                    if job[1] == 2 * KT - 1:
                        for r in range(2):
                            sp.wait_ge(v_stored[r], 16 * ((KT + 1 - r) // 2))
                        sp.dma_start(vp[0][:, :, :], v_dram[0]).then_inc(v_loaded, 16)
                elif job == ("K", 3):
                    copy_k(0, 0)
                elif job[0] == "Q":
                    copy_q(0, 0, slice(job[1] * QW, (job[1] + 1) * QW), job[1] + 1, q0_copied[job[1]])
                elif job == ("MX", 0):
                    sp.wait_ge(init, 11)
                    set_shift(0, 0, 0)
                elif job[0] == "MX":
                    set_shift(0, 0, 1)

            def load_ot(b):
                sp.dma_start(otb[:, :, :], o_dram[:, :, bass.ds(b * QW, QW)].rearrange("k p q -> p k q")).then_inc(ot_loaded, 16)

            def body(pair, plan, first, last):
                n, half, u = pair
                nn, nhalf, nu = after(pair)

                def store_o(n, qb):
                    sp.wait_ge(norm_done, 2 + 4 * n + qb + 1)
                    sp.dma_start(o_dram[n, :, qb * QW:(qb + 1) * QW], onorm[:, :]).then_inc(o_stored[qb % 2], 16)

                if not last:
                    sp.wait_ge(q_lo, 8 * (n + 1))
                    sp.wait_ge(k_lo, 8 * (n + 1))
                    load_pair_weights(sp, nn, nu)
                    copy_q(nn, nu, slice(0, SEQ), 4, q_copied)
                    if not first:
                        store_o(n - 1, QB - 1)
                        sp.wait_ge(pv_done, CREDIT + STEPS * n)
                    copy_k(nn, nu)
                    sp.dma_start(vp[nu][:, :, :], v_dram[nn]).then_inc(v_loaded, 16)
                else:
                    store_o(n - 1, QB - 1)
                    sp.wait_ge(pv_done, CREDIT + STEPS * n)
                    sp.dma_start(k0raw[:, :, :], k0.rearrange("(c p) n -> p c n", p=P)).then_inc(ld_raw, 16)
                    sp.dma_start(k2raw[:, :, :], k2.rearrange("(c p) n -> p c n", p=P)).then_inc(ld_raw, 16)
                    sp.dma_start(k1raw[:, :, :], k1.rearrange("(c p) n -> p c n", p=P)).then_inc(ld_raw, 16)
                    sp.dma_start(wo_sb[:, :, :], wout.rearrange("(c p) n -> p c n", p=P)).then_inc(ld_tail, 16)
                    sp.dma_start(xres[:, :, :], x[0].rearrange("(t p) d -> p t d", p=P)).then_inc(ld_tail, 16)
                    sp.dma_start(gout[:, :], g_out.unsqueeze(0).broadcast_to([P, DIM])).then_inc(ld_tail, 16)
                store_o(n, 0)
                if not last:
                    if first:
                        sp.wait_ge(init, 17)
                    set_shift(nn, nu, 0)
                else:
                    sp.wait_ge(o_stored[0], 16 * 2 * PAIRS)
                    load_ot(0)
                store_o(n, 1)
                store_o(n, 2)
                if not last:
                    set_shift(nn, nu, 1)
                else:
                    sp.wait_ge(y0_var, 2)
                    sp.wait_ge(o_stored[1], 16 * 2 * PAIRS)
                    load_ot(1)
                    store_o(n, 3)

            pair_loop(sp, body)

            def store_out(b):
                for h in range(2):
                    sp.wait_ge(res_made, 4 * b + 2 * h + 2)
                    sp.dma_start(out[0, bass.ds(b * QW + h * 2 * P, 2 * P), :].rearrange("(t p) d -> p t d", p=P),
                                 obuf[h][:, :, :]).then_inc(out_stored[h], 16)

            for r in range(2):
                sp.wait_ge(o_stored[r], 16 * (1 + 2 * PAIRS))
            with sp.Fori(0, QB - 2) as b:
                sp.wait_ge(c_made, 4 * b + 4)
                load_ot(b + 2)
                store_out(b)
            store_out(QB - 2)
            store_out(QB - 1)
            for r in range(2):
                sp.wait_ge(out_stored[r], 16 * (1 + QB))

        @block.gpsimd
        def _(gp):
            gp.memset(ctxA[:, NULL_TILE, :], 0.0).then_inc(clear_ctx, 1)
            gp.memset(mask8[:, :], 0).then_inc(clear_ctx, 1)
            gp.memset(ident[:, :], 0.0).then_inc(ident_made, 1)
            gp.wait_ge(ident_made, 1)
            gp.affine_select(out=ident[:, :], in_=ident[:, :], compare_op=ALU.not_equal, fill=1.0, base=0,
                             pattern=[[-1, P]], channel_multiplier=1).then_inc(ident_made, 1)
            gp.memset(ones[:, :], 1.0).then_inc(init, 1)
            gp.wait_ge(init, 1)
            gp.wait_ge(ident_made, 2)
            gp.wait_ge(clear_ctx, 2)
            gp.memset(wv1[CDIM - P:C1, :], 0.0).then_inc(init, 1)
            for u in range(2):
                gp.memset(wkp1[u][CDIM - P:C1, :], 0.0).then_inc(init, 1)
            gp.wait_ge(init, 4)
            gp.memset(epscol[:, :], EPS)
            gp.memset(minus_half[:, :], -0.5).then_inc(half_made, 1)
            gp.memset(eps2col[:, :], EPS * EPS).then_inc(init, 1)
            gp.memset(ctxA[:, 0:NULL_TILE, CDIM + 1:CAUG], 0.0).then_inc(null_set, 1)
            gp.wait_ge(clear_ctx, 1)
            gp.affine_select(out=ctxA[:, NULL_TILE, CDIM + 1:CAUG], in_=ctxA[:, NULL_TILE, CDIM + 1:CAUG],
                             compare_op=ALU.not_equal, fill=1.0, base=-NULL_ROW, pattern=[[0, 1]],
                             channel_multiplier=1).then_inc(null_set, 1)

            def clear_operands(u):
                gp.wait_ge(init, 5 + 6 * u)
                gp.wait_ge(null_set, 2)
                for g in range(2):
                    gp.wait_ge(init, 5 + 6 * u + 2 * g)
                    gp.memset(qrest[u][g][lo_rows(g), :].bitcast(F32), 0.0).then_inc(init, 1)
                    gp.memset(krest[u][g][lo_rows(g), :].bitcast(F32), 0.0).then_inc(init, 1)
                gp.wait_ge(init, 9 + 6 * u)
                for g in range(2):
                    gp.wait_ge(init, 9 + 6 * u + g)
                    r = shift_row(g)
                    gp.memset(krest[u][g][r:r + 1, :].bitcast(F32), 1.0).then_inc(init, 1)

            clear_operands(0)
            for r in range(2):
                gp.wait_ge(v_stored[r], 16 * ((KT + 1 - r) // 2))
            gp.wait_ge(tr_free, CT_N + XT_N)
            gp.wait_ge(vh_free, 2 * KT)
            gp.wait_ge(keybias_made, 2)
            clear_operands(1)
            gp.wait_ge(init, 17)

            def body(pair, plan, first, last):
                n, half, u = pair

                for s in range(STEPS):
                    for g in range(2):
                        if s % KT and gpsimd_sums(g, s, last):
                            add_tile(gp, n, s, g)
                    if last and s in (C_STEP + 4, C_STEP + 8):
                        r = (s - C_STEP - 4) // 4
                        gp.wait_ge(half_made, 1)
                        gp.wait_ge(y0_var, 2 + r)
                        gp.tensor_scalar(y0var[r][:, :], y0mv[r][:, :, 1], EPS, None, ALU.add).then_inc(y0_root, 1)
                        gp.wait_ge(y0_root, 2 * r + 1)
                        gp.tensor_tensor(y0rs[r][:, :], y0var[r][:, :], minus_half[:, :], ALU.pow).then_inc(y0_root, 1)
                if last:
                    gp.wait_ge(ld_raw, 48)
                    gp.wait_ge(pv_done, CREDIT + STEPS * PAIRS)
                    for k in range(FK):
                        gp.tensor_scalar(w1[:, k, :], k1raw[:, k, :], 2.0, -1.0, ALU.mult, ALU.add).then_inc(w1_made, 1)

            gp.sem_inc(o_stored[0], 16)
            gp.sem_inc(o_stored[1], 16)
            gp.sem_inc(sum_done[0], CREDIT)
            pair_loop(gp, body)

            def root(i, r, n):
                gp.wait_ge(cv_made, n + 1)
                gp.tensor_tensor(cve[i % 2][:, r:r + 1], cmv[i % 2][:, r, 1:2], epscol[:, :], ALU.add).then_inc(cve_made, 1)
                gp.wait_ge(cve_made, n + 1)
                gp.tensor_tensor(crs[i % 2][:, r:r + 1], cve[i % 2][:, r:r + 1], minus_half[:, 0:1], ALU.pow).then_inc(crs_made, 1)

            def roots(b):
                for k in range(5):
                    if k < 4:
                        root(k, 0, 8 * (b - 1) + ROOT[("A", k)])
                    if k >= 1:
                        root(k - 1, 1, 8 * (b - 1) + ROOT[("B", k - 1)])

            with gp.Fori(0, QB - 1) as b:
                roots(b + 1)

        @block.scalar
        def _(act):
            act.sem_inc(p_made[0], 1)
            act.sem_inc(p_made[1], 1)
            act.sem_inc(f_free, 3)

            def wait_side(j, pair):
                slot, before = slot_of(j, pair)
                act.wait_ge(side_made[slot], before + 1)
                return slot

            def side(j, job, pair):
                nxt, _, nu = after(pair)
                if job[0] == "K":
                    if job[1] == 0 and pair is not None:
                        for r in range(2):
                            act.wait_ge(v_stored[r], 16 * ((KT + 1 - r) // 2))
                        act.wait_ge(keybias_made, 2)
                    slot = wait_side(j, pair)
                    cols = slice(job[1] * KCH, (job[1] + 1) * KCH)
                    for g in range(2):
                        act.activation(khl[nu][g][hi_rows(g), cols], ps_side[slot][hi_rows(g), 0, 0:KCH],
                                       ACT.Copy).then_inc(k_hi, 1)
                    if job[1] == 0:
                        act.wait_ge(w_loaded[nu], 48 * (after(pair)[1] + 1))
                        if pair is not None:
                            act.wait_ge(q_lo, 8 * nxt)
                        act.activation(wq_hi[:, :, :], wqp[:, :, :], ACT.Copy).then_inc(wq_rounded, 1)
                elif job[0] == "Q":
                    slot = wait_side(j, pair)
                    cols = slice(job[1] * QW, (job[1] + 1) * QW)
                    for g in range(2):
                        act.activation(qdup[nu][g][hi_rows(g), cols], ps_side[slot][hi_rows(g), 0, :],
                                       ACT.Copy).then_inc(q_hi, 1)
                elif job[0] == "MX":
                    slot = wait_side(j, pair)
                    g = job[1]
                    act.wait_ge(shift_set, 32 * nxt)
                    act.activation(rowbuf[g][:, :], ps_side[slot][0:QT, 0, 0:P], ACT.Copy,
                                   scale=-1.0).then_inc(row_made[g], 1)
                    act.wait_ge(row_made[g], nxt + 1)
                    act.sem_inc(side_free[slot], 1)

            def evac_v(h):
                kt, half = h // 2, h % 2
                act.wait_ge(vh_made, h + 1)
                if half == 0 and kt >= 2:
                    act.wait_ge(v_stored[kt % 2], 16 * (kt // 2))
                act.activation(vsb[kt % 2][:, half * 512:(half + 1) * 512], ps_o[h % 2][:, :],
                               ACT.Copy).then_inc(vh_free, 1)

            roots = iter(range(4))

            def root():
                c = next(roots)
                act.wait_ge(ln_var, c + 1)
                act.activation(sd[:, 4 * c:4 * c + 4], mv[:, 4 * c:4 * c + 4, 1], ACT.Sqrt, scale=1.0 + EPS,
                               bias=eps2col[:, :]).then_inc(ln_sd, 1)

            act.wait_ge(init, 5)
            act.activation(preload[:, 0:1], epscol[:, :], ACT.Sqrt)
            for n, job in HEAD:
                if job[0] == "CT":
                    i = job[1]
                    tiles = min(2, KT - 2 * i)
                    cols = slice(2 * i * P, (2 * i + tiles) * P)
                    act.wait_ge(tr_made, i + 1)
                    act.activation(cT0[:, cols], ps_s[i % 2][:, 0:tiles * P], ACT.Copy)
                    act.activation(cT1[:, cols], ps_s[i % 2][0:C1, 2 * P:(2 + tiles) * P], ACT.Copy).then_inc(tr_free, 1)
                    if i >= CT_N - 2:
                        root()
                elif job[0] == "XT":
                    t = 2 * job[1]
                    i = CT_N + job[1]
                    act.wait_ge(tr_made, i + 1)
                    for c in range(DC):
                        copied = act.activation(x_hi[:, c, t * P:(t + 2) * P], ps_s[i % 2][:, c * 2 * P:(c + 1) * 2 * P],
                                                ACT.Copy, scale=gcol[:, c:c + 1])
                    copied.then_inc(x_rounded, 1)
                elif job[0] == "V":
                    if job[2]:
                        evac_v(job[1])
                else:
                    side(n, job, None)
                    if job in (("K", 1), ("K", 2)):
                        root()
                    if job == ("K", 3):
                        act.wait_ge(gcol_made, 1)

            def body(pair, plan, first, last):
                n, half, u = pair

                for s in range(STEPS):
                    kt = s % KT
                    freed = consumed(s - RING) + CREDIT if s >= RING else consumed(STEPS + s - RING) + CREDIT - (KT - 1) * QB
                    for g in range(2):
                        act.wait_ge(s_made[g], STEPS * n + s + 1)
                        act.wait_ge(pv_done, STEPS * n + s + 1)
                        act.wait_ge(sum_done[g], (KT - 1) * QB * n + freed)
                        act.activation(prob[g][s % RING][:, :], ps_s[g][:, :], ACT.Exp,
                                       bias=keybias[:, kt:kt + 1], scale=SCALE).then_inc(p_made[g], 1)
                    for j, job in plan[s]:
                        side(j, job, pair)
                if last:
                    act.wait_ge(pv_done, CREDIT + STEPS * PAIRS)
                    act.activation(fT[0][:, :], ps_o[(QB - 1) % 2][:, :], ACT.Copy).then_inc(o_copied, 1)

            act.activation(preload[:, 1:2], epscol[:, :], ACT.Exp)
            act.wait_ge(keybias_made, 2)
            pair_loop(act, body)

            def round_y(b, t):
                act.wait_ge(t_made, turns_before(b) + t + 1)
                act.activation(yhi[:, :, t * P:(t + 1) * P], ps_t[t % 2][:, 0:DIM].rearrange("p (c q) -> p c q", c=DC),
                               ACT.Copy).then_inc(yhi_made, 1)

            def chain(b, k):
                if 4 <= k < 8:
                    round_y(b, k - 4)

            for t in range(4):
                round_y(0, t)

            def relu(b, j, scale):
                act.wait_ge(f_made, 18 * b + j + 1)
                act.wait_ge(h_free, 16 * b + j + 1)
                if j % 2:
                    act.activation((h0hi if j < 8 else h1hi)[:, j % 8, :], ps_f[j % 3], ACT.Relu, scale=scale)
                act.activation(hf[j % 2][:, :], ps_f[j % 3], ACT.Relu, scale=scale).then_inc(h_made, 1)
                act.wait_ge(h_made, 16 * b + j + 1)
                act.sem_inc(f_free, 1)

            def tail(b, with_next):
                for m in range(8):
                    relu(b, m, scol[:, 0:1])
                for m in range(8):
                    if with_next:
                        chain(b + 1, m)
                    relu(b, 8 + m, scol[:, 1:2])
                act.wait_ge(norm_done, 2 + 4 * PAIRS)
                for m in range(DC):
                    j = 16 + m
                    act.wait_ge(f_made, 18 * b + j + 1)
                    act.activation(fT[m][:, :], ps_f[j % 3], ACT.Copy, scale=s2x8[:, :]).then_inc(fT_made, 1)
                    act.wait_ge(fT_made, DC * b + m + 1)
                    act.sem_inc(f_free, 1)

            act.wait_ge(ld_g, 48)
            act.wait_ge(s2_made, 1)
            with act.Fori(0, QB - 1) as b:
                tail(b, True)
            tail(QB - 1, False)

        @block.vector
        def _(dve):
            dve.sem_inc(sum_done[1], CREDIT)
            dve.sem_inc(norm_done, 2)
            dve.sem_inc(c_free, 2)
            dve.sem_inc(out_stored[0], 16)
            dve.sem_inc(out_stored[1], 16)
            dve.sem_inc(t_free, 2)
            dve.sem_inc(h_free, 2)
            dve.wait_ge(ld_mask, 32)
            dve.tensor_copy(maskf[:, :], mask8[:, :]).then_inc(maskf_made, 1)
            dve.wait_ge(maskT_made, 1)
            dve.tensor_copy(m13[:, :], ps_o[0][:, 0:KT]).then_inc(m13_made, 1)
            dve.wait_ge(m13_made, 1)
            dve.wait_ge(null_set, 2)
            dve.tensor_scalar(ctxA[:, :, CDIM], m13[:, :], -1.0, 1.0, ALU.mult, ALU.add).then_inc(flag_made, 1)
            dve.tensor_tensor(keybias[:, :], m13[:, :], ctxA[:, :, CDIM + 1], ALU.add).then_inc(keybias_made, 1)
            dve.wait_ge(keybias_made, 1)
            dve.tensor_scalar(keybias[:, :], keybias[:, :], -1.0, -MASKED, ALU.add, ALU.mult).then_inc(keybias_made, 1)

            dve.wait_ge(gT_made, 1)
            dve.tensor_copy(gcol[:, :], ps_o[1][:, 0:DC]).then_inc(gcol_made, 1)

            for i in range(CT_N):
                if 2 * i == NULL_TILE:
                    dve.wait_ge(ld_ctx[2], 16)
                elif 2 * i % (NULL_TILE // 2) == 0:
                    dve.wait_ge(ld_ctx[4 * i // NULL_TILE], 16)
                for kt in range(2 * i, min(2 * i + 2, KT)):
                    masked = dve.tensor_scalar(ctxA[:, kt, 0:CDIM], ctxA[:, kt, 0:CDIM], m13[:, kt:kt + 1], None, ALU.mult)
                masked.then_inc(ctx_masked, 1)

            def statistics(c):
                dve.wait_ge(ld_x[c], 16)
                for t in range(4 * c, 4 * c + 4):
                    dve.bn_stats(st[:, t, :], xs[:, t, :]).then_inc(ln_stats, 1)
                dve.wait_ge(ln_stats, 4 * (c + 1))
                for t in range(4 * c, 4 * c + 4):
                    got = dve.bn_aggr(mv[:, t, :], st[:, t, :])
                got.then_inc(ln_var, 1)

            def normalise(c):
                dve.wait_ge(ln_sd, c + 1)
                dve.reciprocal(rs[:, 4 * c:4 * c + 4], sd[:, 4 * c:4 * c + 4]).then_inc(ln_rs, 1)
                dve.wait_ge(ln_rs, c + 1)
                dve.wait_ge(ln_var, c + 1)
                for t in range(4 * c, 4 * c + 4):
                    dve.tensor_scalar(xs[:, t, :], xs[:, t, :], mv[:, t, 0:1], rs[:, t:t + 1],
                                      ALU.subtract, ALU.mult).then_inc(ln_out, 1)

            def invert_half(h):
                slot, before = slot_of(PLAN_LAST[STEPS][0][0], LAST_PAIR)
                cols = slice(h * QW // 2, (h + 1) * QW // 2)
                dve.wait_ge(side_made[slot], before + 1)
                dve.wait_ge(o_stored[0], 16 * (1 + 2 * PAIRS))
                inverted = dve.reciprocal(onorm[:, cols], ps_side[slot][:, 0, cols])
                if h:
                    inverted.then_inc(rec_made, 1)

            def side(j, job, pair):
                nxt, _, nu = after(pair)
                slot, before = slot_of(j, pair)
                if job[0] in "KQ":
                    c = job[1]
                    if job[0] == "K":
                        w, hi, whole, rest, lo_done = KCH, khl, k_hi, khl, k_lo
                    else:
                        w, hi, whole, rest, lo_done = QW, qdup, q_hi, qrest, q_lo
                    cols = slice(c * w, (c + 1) * w)
                    for g in range(2):
                        dve.wait_ge(whole, 8 * nxt + 2 * c + g + 1)
                        rows = lo_rows(g) if job[0] == "K" else hi_rows(g)
                        last = dve.tensor_tensor(rest[nu][g][rows, cols], ps_side[slot][hi_rows(g), 0, 0:w],
                                                 hi[nu][g][hi_rows(g), cols].bitcast(F32), ALU.subtract)
                        last.then_inc(lo_done, 1)
                    dve.wait_ge(lo_done, 8 * nxt + 2 * c + 2)
                    dve.sem_inc(side_free[slot], 1)
                    if job == ("K", 0):
                        dve.wait_ge(wq_rounded, nxt + 1)
                        dve.tensor_tensor(wq_lo[:, :, :], wqp[:, :, :], wq_hi[:, :, :].bitcast(F32), ALU.subtract).then_inc(wq_split, 1)
                elif job[0] == "SA":
                    _, g, qt, half = job
                    dve.wait_ge(side_made[slot], before + 1)
                    dve.reduce_max(mxh[:, g, qt, half:half + 1], ps_side[slot][:, :, 0:MXW], AX.XY).then_inc(side_free[slot], 1)
                    if (qt, half) == (QT - 1, 1):
                        dve.wait_ge(side_free[slot], before + 1)
                        dve.reduce_max(mx[:, g, :], mxh[:, g, :, :], AX.X).then_inc(mx_made, 1)
                elif job[0] == "C":
                    dve.wait_ge(side_made[slot], before + 1)
                    dve.wait_ge(pv_done, CREDIT + STEPS * (PAIRS - 1))
                    for t in range(2 * job[1], 2 * job[1] + 2):
                        dve.bn_stats(y0st[:, t, :], ps_side[slot][:, t % 2, 0:DIM]).then_inc(y0_stats, 1)
                    dve.wait_ge(y0_stats, 2 * job[1] + 2)
                    for t in range(2 * job[1], 2 * job[1] + 2):
                        got = dve.bn_aggr(y0mv[0][:, t, :], y0st[:, t, :])
                    got.then_inc(y0_var, 1)
                elif job[0] in ("L", "LP"):
                    qb = job[1]
                    block = 4 * (pair[0] - 1 if job[0] == "LP" else pair[0]) + qb
                    dve.wait_ge(side_made[slot], before + 1)
                    n = pair[0] - 1 if job[0] == "LP" else pair[0]
                    at_end = job[0] == "L" and qb == QB - 1
                    if at_end:
                        invert_half(1)
                        dve.wait_ge(rec_made, block + 1)
                    else:
                        dve.wait_ge(o_stored[(qb + 1) % 2], 16 * (1 + 2 * n + (qb + 1) // 2))
                        dve.reciprocal(onorm[:, :], ps_side[slot][:, 0, :]).then_inc(rec_made, 1)
                        dve.wait_ge(rec_made, block + 1)
                    dve.sem_inc(side_free[slot], 1)
                    if at_end:
                        dve.wait_ge(o_copied, 1)
                    else:
                        dve.wait_ge(pv_done, CREDIT + KT * (block + 1))
                    dve.tensor_tensor(onorm[:, :], fT[0][:, :] if at_end else ps_o[qb % 2][:, :], onorm[:, :],
                                      ALU.mult).then_inc(norm_done, 1)

            statistics(0)
            statistics(1)
            normalise(0)
            normalise(1)
            beside_k = {0: lambda: statistics(2), 1: lambda: statistics(3), 2: lambda: normalise(2), 3: lambda: normalise(3)}
            for j, job in HEAD:
                if j is not None:
                    side(j, job, None)
                    if job[0] == "K":
                        beside_k[job[1]]()
                elif job[0] == "XT":
                    t = 2 * job[1]
                    i = CT_N + job[1]
                    dve.wait_ge(x_rounded, job[1] + 1)
                    for c in range(DC):
                        cols = slice(t * P, (t + 2) * P)
                        rest = dve.scalar_tensor_tensor(x_lo[:, c, cols], ps_s[i % 2][:, c * 2 * P:(c + 1) * 2 * P], gcol[:, c:c + 1],
                                                        x_hi[:, c, cols].bitcast(F32), ALU.mult, ALU.subtract)
                    rest.then_inc(tr_free, 1)

            def attn_block_0():
                dve.wait_ge(y0_root, 2)
                dve.wait_ge(ld_tail, 48)
                for i in range(2):
                    slot, before = slot_of(C_JOBS[i], LAST_PAIR)
                    for t in range(2 * i, 2 * i + 2):
                        dve.tensor_scalar(y0[:, t, :], ps_side[slot][:, t % 2, 0:DIM], y0mv[0][:, t, 0:1], y0rs[0][:, t:t + 1],
                                          ALU.subtract, ALU.mult).then_inc(y0_step, 1)
                for i in range(2):
                    slot, before = slot_of(C_JOBS[i], LAST_PAIR)
                    dve.wait_ge(y0_step, 2 * i + 2)
                    dve.sem_inc(side_free[slot], 1)
                for t in range(4):
                    dve.tensor_tensor(y0[:, t, :], y0[:, t, :], gout[:, :], ALU.mult).then_inc(y0_step, 1)
                dve.wait_ge(y0_step, 8)
                dve.tensor_tensor(xres[:, 0:4, :], xres[:, 0:4, :], y0[:, :, :], ALU.add).then_inc(y0_step, 1)
                dve.wait_ge(y0_step, 9)
                for t in range(4):
                    dve.bn_stats(y0st[:, t, :], xres[:, t, :]).then_inc(y0_stats, 1)
                dve.wait_ge(y0_stats, 8)
                for t in range(4):
                    got = dve.bn_aggr(y0mv[1][:, t, :], y0st[:, t, :])
                got.then_inc(y0_var, 1)

            def body(pair, plan, first, last):
                n, half, u = pair
                for s in range(STEPS):
                    for j, job in plan[s]:
                        side(j, job, pair)
                    for g in range(2):
                        if s % KT and not gpsimd_sums(g, s, last):
                            add_tile(dve, n, s, g)
                    if last and s == C_STEP + 4:
                        attn_block_0()
                    if last and s == C_STEP + 8:
                        dve.wait_ge(y0_root, 4)
                        for t in range(4):
                            dve.tensor_scalar(y0[:, t, :], xres[:, t, :], y0mv[1][:, t, 0:1], y0rs[1][:, t:t + 1],
                                              ALU.subtract, ALU.mult).then_inc(y0_made, 1)
                    if last and s == 20:
                        dve.wait_ge(ld_raw, 48)
                        dve.wait_ge(ld_g, 48)
                        dve.tensor_tensor(w0[:, :, :], k0raw[:, 0:DC, :], k0raw[:, DC:2 * DC, :], ALU.subtract).then_inc(w_small_made, 1)
                        dve.tensor_scalar(w2[:, :, :], k2raw[:, :, :], 2.0, -1.0, ALU.mult, ALU.add).then_inc(w_small_made, 1)
                        dve.tensor_scalar(s2x8[:, :], scol[:, 2:3], 8.0, None, ALU.mult).then_inc(s2_made, 1)

            pair_loop(dve, body)

            def chain(b, k):
                base = CHAIN_N * (b - 1)

                def step(instruction, key):
                    instruction.then_inc(cstep, 1)
                    dve.wait_ge(cstep, base + ORDER[key])

                if k < 4:
                    i = k
                    dve.wait_ge(c_made, 4 * (b - 1) + i + 1)
                    step(dve.bn_stats(cst[i % 2][:, 0, :], ps_c[i % 2][:, 0:DIM]), ("A1", i))
                    dve.sem_inc(stood, 1)
                    dve.bn_aggr(cmv[i % 2][:, 0, :], cst[i % 2][:, 0, :]).then_inc(cv_made, 1)
                if 1 <= k < 5:
                    i = k - 1
                    dve.wait_ge(crs_made, 8 * (b - 1) + ROOT[("A", i)] + 1)
                    dve.tensor_scalar(attn[i % 2][:, :], ps_c[i % 2][:, 0:DIM], cmv[i % 2][:, 0, 0:1], crs[i % 2][:, 0:1],
                                      ALU.subtract, ALU.mult).then_inc(c_free, 1)
                    dve.wait_ge(c_free, 2 + 4 * (b - 1) + i + 1)
                    step(dve.tensor_tensor(attn[i % 2][:, :], attn[i % 2][:, :], gout[:, :], ALU.mult), ("B2", i))
                    xr = xres[:, bass.ds(4 * b + i, 1), :].rearrange("p a d -> p (a d)")
                    step(dve.tensor_tensor(xr, xr, attn[i % 2][:, :], ALU.add), ("B3", i))
                    dve.sem_inc(stood, 1)
                    step(dve.bn_stats(cst[i % 2][:, 1, :], xr), ("B4", i))
                    dve.sem_inc(stood, 1)
                    dve.bn_aggr(cmv[i % 2][:, 1, :], cst[i % 2][:, 1, :]).then_inc(cv_made, 1)
                if 2 <= k < 6:
                    i = k - 2
                    dve.wait_ge(crs_made, 8 * (b - 1) + ROOT[("B", i)] + 1)
                    xr = xres[:, bass.ds(4 * b + i, 1), :].rearrange("p a d -> p (a d)")
                    if i >= 2:
                        dve.wait_ge(t_made, turns_before(b) + i - 1)
                    dve.tensor_scalar(ysb[i % 2][:, :], xr, cmv[i % 2][:, 1, 0:1], crs[i % 2][:, 1:2],
                                      ALU.subtract, ALU.mult).then_inc(y_made, 1)
                if 4 <= k < 8:
                    rest_of_y(b, k - 4)

            def rest_of_y(b, t):
                dve.wait_ge(yhi_made, 4 * b + t + 1)
                dve.tensor_tensor(ylo[:, :, t * P:(t + 1) * P], ps_t[t % 2][:, 0:DIM].rearrange("p (c q) -> p c q", c=DC),
                                  yhi[:, :, t * P:(t + 1) * P].bitcast(F32), ALU.subtract).then_inc(y_split, 1)
                dve.wait_ge(y_split, 4 * b + t + 1)
                dve.sem_inc(t_free, 1)

            dve.wait_ge(pv_done, CREDIT + STEPS * PAIRS)
            for i in range(4):
                rest_of_y(0, i)

            def split(b, j):
                hi, lo = (h0hi, h0lo) if j < 8 else (h1hi, h1lo)
                dve.wait_ge(h_made, 16 * b + j + 1)
                if j % 2 == 0:
                    dve.tensor_copy(hi[:, j % 8, :], hf[j % 2][:, :]).then_inc(split_step, 1)
                    dve.wait_ge(split_step, 8 * b + j // 2 + 1)
                dve.tensor_tensor(lo[:, j % 8, :], hf[j % 2][:, :], hi[:, j % 8, :].bitcast(F32),
                                  ALU.subtract).then_inc(h_free, 1)

            def tail(b, with_next):
                for j in range(2, 8):
                    split(b, j)
                for j in range(8):
                    if with_next:
                        chain(b + 1, j)
                    split(b, 8 + j)
                for t in range(4):
                    dve.wait_ge(t_made, 8 * b + (8 if with_next else 4) + t + 1)
                    dve.wait_ge(out_stored[t // 2], 16 * (1 + b))
                    xr = xres[:, bass.ds(4 * b + t, 1), :].rearrange("p a d -> p (a d)")
                    dve.tensor_tensor(obuf[t // 2][:, t % 2, :], ps_t[t % 2][:, 0:DIM], xr, ALU.add).then_inc(res_made, 1)
                    dve.wait_ge(res_made, 4 * b + t + 1)
                    dve.sem_inc(t_free, 1)
                if with_next:
                    for j in range(2):
                        split(b + 1, j)

            invert_half(0)
            for j in range(2):
                split(0, j)
            side(*PLAN_LAST[STEPS][0], LAST_PAIR)
            with dve.Fori(0, QB - 1) as b:
                tail(b, True)
            tail(QB - 1, False)

        @block.tensor
        def _(pe):
            pe.sem_inc(pv_done, CREDIT)

            pe.wait_ge(maskf_made, 1)
            pe.wait_ge(ident_made, 2)
            pe.transpose(ps_o[0][:, 0:KT], maskf[:, :], ident[0:KT, 0:KT]).then_inc(maskT_made, 1)
            pe.wait_ge(ld_gn, 16)
            pe.transpose(ps_o[1][:, 0:DC], grow[:, :], ident[0:DC, 0:DC]).then_inc(gT_made, 1)
            def project_v(h, part):
                kt, half = h // 2, h % 2
                keys, cols = slice(kt * P, (kt + 1) * P), slice(half * 512, (half + 1) * 512)
                if part == 0:
                    if h == 0:
                        pe.wait_ge(ld_wv, 32)
                        pe.wait_ge(ld_null_v, 16)
                    if h < 2:
                        pe.wait_ge(m13_made, 1)
                        pe.wait_ge(gcol_made, 1)
                    else:
                        pe.wait_ge(vh_free, h - 1)
                    pe.matmul(ps_o[h % 2][:, :], cT0[:, keys], wv0[:, cols], start=True, stop=False)
                else:
                    pe.matmul(ps_o[h % 2][:, :], cT1[:, keys], wv1[:, cols], start=False, stop=True).then_inc(vh_made, 1)

            def side(j, job, pair):
                nxt, nhalf, nu = after(pair)
                slot, before = slot_of(j, pair)
                if not (pair is None and before == 0):
                    pe.wait_ge(side_free[slot], before)
                ps = ps_side[slot]
                if job[0] in "KQ" and job[1] == 0:
                    pe.wait_ge(w_loaded[nu], 48 * (nhalf + 1))
                    if pair is None:
                        pe.wait_ge(ld_null_k, 32)
                if job[0] == "K":
                    cols = slice(job[1] * KCH, (job[1] + 1) * KCH)
                    pe.matmul(ps[:, 0, 0:KCH], wkp0[nu][:, :], cT0[:, cols], start=True, stop=False)
                    pe.matmul(ps[:, 0, 0:KCH], wkp1[nu][:, :], cT1[:, cols], start=False, stop=True).then_inc(side_made[slot], 1)
                elif job[0] == "Q":
                    if pair is None:
                        pe.wait_ge(tr_free, CT_N + 2 * job[1] + 2)
                    cols = slice(job[1] * QW, (job[1] + 1) * QW)
                    if job[1] == 0:
                        pe.wait_ge(wq_split, nxt + 1)
                    terms = [(w, c, part) for w, part in ((wq_hi, x_hi), (wq_hi, x_lo), (wq_lo, x_hi)) for c in range(DC)]
                    for i, (w, c, part) in enumerate(terms):
                        last = pe.matmul(ps[:, 0, :], w[:, c, :], part[:, c, cols], start=(i == 0), stop=(i == len(terms) - 1))
                    last.then_inc(side_made[slot], 1)
                elif job[0] == "SA":
                    _, g, qt, half = job
                    if pair is None and qt % 4 == 0 and half == 0:
                        pe.wait_ge(q0_copied[qt // 4], 32)
                    elif (g, qt, half) == (0, 0, 0):
                        pe.wait_ge(q_copied, 32 * nxt)
                    if (g, qt, half) == (0, 0, 0):
                        pe.wait_ge(k_lo, 8 * (nxt + 1))
                    for j in range(2):
                        cols = slice(half * MXH + j * MXW, half * MXH + (j + 1) * MXW)
                        last = pe.matmul(ps[:, j, 0:MXW], qdup[nu][g][:, qt * P:(qt + 1) * P], khl[nu][g][:, cols],
                                         start=True, stop=True)
                    last.then_inc(side_made[slot], 1)
                elif job[0] == "C":
                    if job[1] == 0:
                        pe.wait_ge(ot_loaded, 16)
                        pe.wait_ge(ld_tail, 48)
                    for t in range(2 * job[1], 2 * job[1] + 2):
                        for k in range(PAIRS):
                            last = pe.matmul(ps[:, t % 2, 0:DIM], otb[:, k, t * P:(t + 1) * P], wo_sb[:, k, :],
                                             start=(k == 0), stop=(k == PAIRS - 1))
                    last.then_inc(side_made[slot], 1)
                elif job[0] == "MX":
                    g = job[1]
                    pe.wait_ge(mx_made, 2 * nxt + g + 1)
                    pe.transpose(ps[0:QT, 0, 0:P], mx[:, g, :], ident[:, :]).then_inc(side_made[slot], 1)
                else:
                    qb = job[1]
                    block = QB * (pair[0] - 1 if job[0] == "LP" else pair[0]) + qb
                    for g in range(2):
                        pe.wait_ge(sum_done[g], CREDIT + (KT - 1) * (block + 1))
                        last = pe.matmul(ps[g * HD:(g + 1) * HD, 0, :], ones[:, :], acc[g][qb % 2][:, :], start=True, stop=True)
                    last.then_inc(side_made[slot], 1)

            for n, job in HEAD:
                if job[0] == "CT":
                    i = job[1]
                    if i == 0:
                        pe.wait_ge(flag_made, 1)
                    pe.wait_ge(ctx_masked, i + 1)
                    if i >= 2:
                        pe.wait_ge(tr_free, i - 1)
                    for k in range(min(2, KT - 2 * i)):
                        pe.transpose(ps_s[i % 2][:, k * P:(k + 1) * P], ctxA[:, 2 * i + k, 0:P], ident[:, :])
                        last = pe.transpose(ps_s[i % 2][0:C1, (2 + k) * P:(3 + k) * P], ctxA[:, 2 * i + k, P:CAUG], ident[:, :])
                    last.then_inc(tr_made, 1)
                    if i == CT_N - 1:
                        pe.wait_ge(tr_free, CT_N)
                elif job[0] == "XT":
                    t = 2 * job[1]
                    i = CT_N + job[1]
                    if t % 4 == 0:
                        pe.wait_ge(ln_out, t + 4)
                    pe.wait_ge(tr_free, i - 1)
                    for c in range(DC):
                        for k in range(2):
                            last = pe.transpose(ps_s[i % 2][:, (2 * c + k) * P:(2 * c + k + 1) * P],
                                                xs[:, t + k, c * P:(c + 1) * P], ident[:, :])
                    last.then_inc(tr_made, 1)
                elif job[0] == "V":
                    project_v(*job[1:])
                else:
                    side(n, job, None)
            pe.wait_ge(vh_free, 2 * KT)

            def values(n, u, s):
                qb, kt = s // KT, s % KT
                if kt == 0:
                    pe.wait_ge(norm_done, 4 * n + qb + 1)
                for g in range(2):
                    pe.wait_ge(p_made[g], 1 + STEPS * n + s + 1)
                    last = pe.matmul(ps_o[qb % 2][hi_rows(g), :], vp[u][:, kt, hi_rows(g)], prob[g][s % RING][:, :],
                                     start=(kt == 0), stop=(kt == KT - 1))
                last.then_inc(pv_done, 1)

            def body(pair, plan, first, last):
                n, half, u = pair
                pe.wait_ge(k_copied, 32 * (n + 1))
                pe.wait_ge(q_lo, 8 * (n + 1))
                pe.wait_ge(shift_set, 32 * (n + 1))
                if u == 0:
                    pe.wait_ge(init, 11)
                else:
                    pe.wait_ge(init, 17)

                for s in range(STEPS):
                    qb, kt = s // KT, s % KT
                    qs, ks = slice(qb * QW, (qb + 1) * QW), slice(kt * P, (kt + 1) * P)
                    for g in range(2):
                        pe.wait_ge(p_made[g], 1 + STEPS * n + s)
                        pe.matmul(ps_s[g][:, :], khl[u][g][:, ks], qdup[u][g][:, qs], start=True, stop=False)
                        pe.matmul(ps_s[g][:, :], krest[u][g][:, ks], qrest[u][g][:, qs], start=False,
                                  stop=True).then_inc(s_made[g], 1)
                    for j, job in plan[s]:
                        side(j, job, pair)
                    if s:
                        values(n, u, s - 1)
                    elif not first:
                        values(n - 1, 1 - u, STEPS - 1)
                    if s == 0:
                        pe.wait_ge(v_loaded, 16 * (n + 1))
                if last:
                    values(n, u, STEPS - 1)

            pair_loop(pe, body)

            def project_out(b, t):
                if t == 0:
                    pe.wait_ge(ot_loaded, 16 * (b + 1))
                pe.wait_ge(c_free, 4 * (b - 1) + t + 1)
                for k in range(PAIRS):
                    last = pe.matmul(ps_c[t % 2][:, 0:DIM], otb[:, k, t * P:(t + 1) * P], wo_sb[:, k, :],
                                     start=(k == 0), stop=(k == PAIRS - 1))
                last.then_inc(c_made, 1)

            def turn_y(b, t, tile):
                pe.wait_ge(t_free, turns_before(b) + t + 1)
                for c in range(DC):
                    last = pe.transpose(ps_t[t % 2][:, c * P:(c + 1) * P], tile[:, c * P:(c + 1) * P], ident[:, :])
                last.then_inc(t_made, 1)

            def chain(b, k):
                if k < 4:
                    project_out(b, k)
                else:
                    t = k - 4
                    pe.wait_ge(y_made, 4 * (b - 1) + t + 1)
                    turn_y(b, t, ysb[t % 2])

            side(*PLAN_LAST[STEPS][0], LAST_PAIR)
            pe.wait_ge(y0_made, 4)
            for t in range(4):
                if t == 0:
                    pe.wait_ge(norm_done, 2 + 4 * PAIRS - 1)
                elif t == 1:
                    pe.wait_ge(o_copied, 1)
                turn_y(0, t, y0[:, t, :])
            pe.wait_ge(side_free[0], TOTAL_N // 2)
            pe.wait_ge(side_free[1], TOTAL_N // 2 - 1)
            pe.wait_ge(w_small_made, 2)

            def layer(b, j, weights, m, hi, lo, depth, inputs_split=None):
                pe.wait_ge(f_free, 18 * b + j + 1)
                for k in range(depth):
                    if inputs_split is not None:
                        pe.wait_ge(h_free, 2 + inputs_split + k + 1)
                    for part in (hi, lo):
                        last = pe.matmul(ps_f[j % 3], weights[:, k, m * P:(m + 1) * P], part[:, k, :],
                                         start=(k == 0 and part is hi), stop=(k == depth - 1 and part is lo))
                last.then_inc(f_made, 1)

            def first_tiles(b):
                pe.wait_ge(y_split, 4 * b + 4)
                for m in range(2):
                    layer(b, m, w0, m, yhi, ylo, DC)

            def tail(b, with_next):
                for m in range(2, 8):
                    layer(b, m, w0, m, yhi, ylo, DC)
                for m in range(8):
                    if with_next:
                        chain(b + 1, m)
                    if m == 0:
                        pe.wait_ge(w1_made, FK)
                    layer(b, 8 + m, w1, m, h0hi, h0lo, FK, 16 * b if m == 0 else None)
                for m in range(DC):
                    layer(b, 16 + m, w2, m, h1hi, h1lo, FK, 16 * b + 8 if m == 0 else None)
                if with_next:
                    first_tiles(b + 1)
                pe.wait_ge(fT_made, DC * (b + 1))
                for t in range(4):
                    pe.wait_ge(t_free, 8 * b + (8 if with_next else 4) + t + 1)
                    for c in range(DC):
                        last = pe.transpose(ps_t[t % 2][:, c * P:(c + 1) * P], fT[c][:, t * P:(t + 1) * P], ident[:, :])
                    last.then_inc(t_made, 1)

            first_tiles(0)
            with pe.Fori(0, QB - 1) as b:
                tail(b, True)
            tail(QB - 1, False)


_INS = ["x", "ctx_768", "mask_BxS2_bf1", "L0_xattn_g_norm", "L0_xattn_null_kv", "L0_xattn_Wq", "L0_xattn_Wkv",
        "L0_xattn_Wout", "L0_xattn_g_out", "L0_ffn_k0", "L0_ffn_k1", "L0_ffn_k2", "L0_ffn_s0", "L0_ffn_s1", "L0_ffn_s2"]


def kernel(**inputs):
    import numpy as np
    import concourse.bacc as bacc
    from concourse.bass_utils import run_bass_kernel_spmd

    nc = bacc.Bacc("TRN2", target_bir_lowering=False, num_devices=1)
    arrays, args = {}, []
    for name in _INS:
        a = np.ascontiguousarray(inputs[name])
        if a.ndim == 0:
            a = a.reshape(1)
        arrays[f"in_{name}"] = a
        args.append(nc.dram_tensor(f"in_{name}", a.shape, mybir.dt.from_np(a.dtype), kind="ExternalInput").ap())
    out = nc.dram_tensor("out", (1, SEQ, DIM), F32, kind="ExternalOutput").ap()
    xattn_ffn_kernel(nc, *args, out)
    r = run_bass_kernel_spmd(nc, [arrays], core_ids=[0])
    return r.results[0]["out"]
```
